# Optimizing a Trainium2 kernel written in Bass

```python
import numpy as np
import jax
import jax.numpy as jnp

def _softmax(x, axis=-1):
    return jax.nn.softmax(x, axis=axis)

def _gelu(x):
    return jax.nn.gelu(x, approximate=True)

def _silu(x):
    return jax.nn.silu(x)

def _sigmoid(x):
    return jax.nn.sigmoid(x)

def _layernorm(x, axis=-1, eps=1e-05):
    m = jnp.mean(x, axis=axis, keepdims=True)
    v = jnp.var(x, axis=axis, keepdims=True)
    return (x - m) / jnp.sqrt(v + eps)

def _scatter_add(tgt, idx, src, axis=0):
    return tgt.at[idx].add(src)

def _segment_sum(src, seg, n):
    return jax.ops.segment_sum(src, seg, n)
kernel_name = 'mk_gnn_ffn_d2_gnn_r8_1d7e40'

def setup_inputs(seed: int=0):
    np.random.seed(seed)
    _w = jnp.asarray

    def _rec_inputs():
        import jax
        import jax.numpy as jnp
        _gk = jax.random.key(seed)
        x = -0.0003713 + 1 * jax.random.normal(jax.random.fold_in(_gk, 1), (6250, 256), jnp.float32)
        _s = jax.random.randint(jax.random.fold_in(_gk, 2), (100000,), 0, 6250, jnp.int32)
        _d = jax.random.randint(jax.random.fold_in(_gk, 3), (100000,), 0, 6250, jnp.int32)
        _loop = jnp.arange(6250, dtype=jnp.int32)
        src = jnp.concatenate([_s, _d, _loop])
        dst = jnp.concatenate([_d, _s, _loop])
        _o = jnp.argsort(dst, stable=True)
        src = src[_o]
        dst = dst[_o]
        edge_type_8 = jax.random.randint(jax.random.fold_in(_gk, 13), (206250,), 0, 8, jnp.int32)
        edge_weight = jax.random.uniform(jax.random.fold_in(_gk, 14), (206250,), jnp.float32, 0.0, 1)
        return (x, src, dst, edge_type_8, edge_weight)
    x, src, dst, edge_type_8, edge_weight = _rec_inputs()

    def _L0_gnn_setup():
        import jax, jax.numpy as jnp
        import numpy as np
        N_NODES = 6250
        N_EDGES = 100000
        IN_FEAT = 256
        OUT_FEAT = 256
        NUM_RELS = 8
        NUM_BASES = 8
        SUBMAT_IN = IN_FEAT // NUM_BASES
        SUBMAT_OUT = OUT_FEAT // NUM_BASES
        key = jax.random.key(seed)
        k_h, k_w, k_src, k_dst, k_rel, k_norm = jax.random.split(key, 6)
        h = jax.random.normal(k_h, (N_NODES, IN_FEAT), dtype=jnp.float32)
        weight = jax.random.normal(k_w, (NUM_RELS, NUM_BASES * SUBMAT_IN * SUBMAT_OUT), dtype=jnp.float32) * 0.05
        edge_src = jax.random.randint(k_src, (N_EDGES,), 0, N_NODES, dtype=jnp.int32)
        edge_dst = jax.random.randint(k_dst, (N_EDGES,), 0, N_NODES, dtype=jnp.int32)
        edge_rel = jax.random.randint(k_rel, (N_EDGES,), 0, NUM_RELS, dtype=jnp.int32)
        edge_norm = jax.random.uniform(k_norm, (N_EDGES,), dtype=jnp.float32)
        return {'h': h, 'weight': weight, 'edge_src': edge_src, 'edge_dst': edge_dst, 'edge_rel': edge_rel, 'edge_norm': edge_norm}
    _L0_gnn_all = _L0_gnn_setup()
    _L0_gnn_in = {k: v for k, v in _L0_gnn_all.items() if k in ('weight',)}
    del _L0_gnn_all

    def _L0_ffn_setup():
        import math
        import jax, jax.numpy as jnp
        import numpy as np
        CAPACITY_FACTOR = 1.25
        TOP_K = 2
        LN_EPS = 1e-05

        def _layer_norm(x, gamma, beta):
            mu = jnp.mean(x, axis=-1, keepdims=True)
            var = jnp.var(x, axis=-1, keepdims=True)
            return (x - mu) * jax.lax.rsqrt(var + LN_EPS) * gamma + beta
        key = jax.random.key(seed)
        ks = jax.random.split(key, 4)
        B, S, D, F, E = (8, 512, 256, 512, 8)
        x = jax.random.normal(ks[0], (B, S, D), dtype=jnp.float32)
        Wr = jax.random.normal(ks[1], (D, E), dtype=jnp.float32) / np.sqrt(D)
        br = jnp.zeros((E,), jnp.float32)
        W1 = jax.random.normal(ks[2], (E, D, F), dtype=jnp.float32) / np.sqrt(D)
        b1 = jnp.zeros((E, F), jnp.float32)
        W2 = jax.random.normal(ks[3], (E, F, D), dtype=jnp.float32) / np.sqrt(F)
        b2 = jnp.zeros((E, D), jnp.float32)
        gamma = jnp.ones((D,), jnp.float32)
        beta = jnp.zeros((D,), jnp.float32)
        return {'x': x, 'Wr': Wr, 'br': br, 'W1': W1, 'b1': b1, 'W2': W2, 'b2': b2, 'gamma': gamma, 'beta': beta}
    _L0_ffn_all = _L0_ffn_setup()
    _L0_ffn_in = {k: v for k, v in _L0_ffn_all.items() if k in ('Wr', 'br', 'W1', 'b1', 'W2', 'b2', 'gamma', 'beta')}
    del _L0_ffn_all

    def _L1_gnn_setup():
        import jax, jax.numpy as jnp
        import numpy as np
        N = 6250
        E = 100000
        IN_C = 256
        HEADS = 8
        OUT_C = 32
        key = jax.random.key(seed)
        k1, k2, k3, k4, k5 = jax.random.split(key, 5)
        x = jax.random.normal(k1, (N, IN_C), dtype=jnp.float32)
        edge_index = jax.random.randint(k2, (2, E), 0, N, dtype=jnp.int64)
        lim_W = float(np.sqrt(6.0 / (IN_C + HEADS * OUT_C)))
        lim_a = float(np.sqrt(6.0 / (HEADS + OUT_C)))
        W = jax.random.uniform(k3, (IN_C, HEADS * OUT_C), minval=-lim_W, maxval=lim_W, dtype=jnp.float32)
        a_src = jax.random.uniform(k4, (HEADS, OUT_C), minval=-lim_a, maxval=lim_a, dtype=jnp.float32)
        a_dst = jax.random.uniform(k5, (HEADS, OUT_C), minval=-lim_a, maxval=lim_a, dtype=jnp.float32)
        return {'x': x, 'edge_index': edge_index, 'W': W, 'a_src': a_src, 'a_dst': a_dst}
    _L1_gnn_all = _L1_gnn_setup()
    _L1_gnn_in = {k: v for k, v in _L1_gnn_all.items() if k in ('W', 'a_src', 'a_dst')}
    del _L1_gnn_all

    def _L1_ffn_setup():
        import jax, jax.numpy as jnp
        import numpy as np
        BN_EPS = 0.001

        def _bn(h, g, b, m, v):
            return g * (h - m) * jax.lax.rsqrt(v + BN_EPS) + b
        key = jax.random.key(seed)
        ks = jax.random.split(key, 8)
        B, F, Df = (256, 64, 256)
        E, H, D = (8, 256, 256)
        s1 = 1.0 / np.sqrt(Df)
        s2 = 1.0 / np.sqrt(H)
        return {'x': jax.random.normal(ks[0], (B, F, Df), jnp.float32), 'Wr': jax.random.normal(ks[1], (Df, E), jnp.float32) * s1, 'br': jnp.zeros((E,), jnp.float32), 'W1': jax.random.normal(ks[2], (E, Df, H), jnp.float32) * s1, 'b1': jnp.zeros((E, H), jnp.float32), 'g1': jnp.ones((E, H), jnp.float32), 'be1': jnp.zeros((E, H), jnp.float32), 'm1': jnp.zeros((E, H), jnp.float32), 'v1': jnp.ones((E, H), jnp.float32), 'W2': jax.random.normal(ks[3], (E, H, H), jnp.float32) * s2, 'b2': jnp.zeros((E, H), jnp.float32), 'g2': jnp.ones((E, H), jnp.float32), 'be2': jnp.zeros((E, H), jnp.float32), 'm2': jnp.zeros((E, H), jnp.float32), 'v2': jnp.ones((E, H), jnp.float32), 'Wo': jax.random.normal(ks[4], (E, H, D), jnp.float32) * s2, 'bo': jnp.zeros((E, D), jnp.float32)}
    _L1_ffn_all = _L1_ffn_setup()
    _L1_ffn_in = {k: v for k, v in _L1_ffn_all.items() if k in ('Wr', 'br', 'W1', 'b1', 'g1', 'be1', 'm1', 'v1', 'W2', 'b2', 'g2', 'be2', 'm2', 'v2', 'Wo', 'bo')}
    del _L1_ffn_all
    return {'x': x, 'src': src, 'dst': dst, 'edge_type_8': edge_type_8, 'edge_weight': edge_weight, 'L0_gnn_weight': _L0_gnn_in['weight'], 'L0_ffn_Wr': _L0_ffn_in['Wr'], 'L0_ffn_br': _L0_ffn_in['br'], 'L0_ffn_W1': _L0_ffn_in['W1'], 'L0_ffn_b1': _L0_ffn_in['b1'], 'L0_ffn_W2': _L0_ffn_in['W2'], 'L0_ffn_b2': _L0_ffn_in['b2'], 'L0_ffn_gamma': _L0_ffn_in['gamma'], 'L0_ffn_beta': _L0_ffn_in['beta'], 'L1_gnn_W': _L1_gnn_in['W'], 'L1_gnn_a_src': _L1_gnn_in['a_src'], 'L1_gnn_a_dst': _L1_gnn_in['a_dst'], 'L1_ffn_Wr': _L1_ffn_in['Wr'], 'L1_ffn_br': _L1_ffn_in['br'], 'L1_ffn_W1': _L1_ffn_in['W1'], 'L1_ffn_b1': _L1_ffn_in['b1'], 'L1_ffn_g1': _L1_ffn_in['g1'], 'L1_ffn_be1': _L1_ffn_in['be1'], 'L1_ffn_m1': _L1_ffn_in['m1'], 'L1_ffn_v1': _L1_ffn_in['v1'], 'L1_ffn_W2': _L1_ffn_in['W2'], 'L1_ffn_b2': _L1_ffn_in['b2'], 'L1_ffn_g2': _L1_ffn_in['g2'], 'L1_ffn_be2': _L1_ffn_in['be2'], 'L1_ffn_m2': _L1_ffn_in['m2'], 'L1_ffn_v2': _L1_ffn_in['v2'], 'L1_ffn_Wo': _L1_ffn_in['Wo'], 'L1_ffn_bo': _L1_ffn_in['bo']}

def reference(x, src, dst, edge_type_8, edge_weight, L0_gnn_weight, L0_ffn_Wr, L0_ffn_br, L0_ffn_W1, L0_ffn_b1, L0_ffn_W2, L0_ffn_b2, L0_ffn_gamma, L0_ffn_beta, L1_gnn_W, L1_gnn_a_src, L1_gnn_a_dst, L1_ffn_Wr, L1_ffn_br, L1_ffn_W1, L1_ffn_b1, L1_ffn_g1, L1_ffn_be1, L1_ffn_m1, L1_ffn_v1, L1_ffn_W2, L1_ffn_b2, L1_ffn_g2, L1_ffn_be2, L1_ffn_m2, L1_ffn_v2, L1_ffn_Wo, L1_ffn_bo):
    import jax
    import jax.numpy as jnp

    def _L0_gnn_ref(h, weight, edge_src, edge_dst, edge_rel, edge_norm):
        import jax, jax.numpy as jnp
        import numpy as np
        N_NODES = 6250
        N_EDGES = 100000
        IN_FEAT = 256
        OUT_FEAT = 256
        NUM_RELS = 8
        NUM_BASES = 8
        SUBMAT_IN = IN_FEAT // NUM_BASES
        SUBMAT_OUT = OUT_FEAT // NUM_BASES
        'RGCNBlockLayer forward (self_loop=False, bias=None, activation=None).\n\n            Per relation r: agg_r[v] = sum_{(u->v) in rel r} norm_e * h[u]\n            then block-diagonal matmul out_r = blockmm(agg_r, W_r); output = sum_r out_r.\n            '
        N, in_feat = h.shape
        R = weight.shape[0]
        msg = h[edge_src] * edge_norm[:, None]
        seg = edge_rel * N + edge_dst
        agg = jax.ops.segment_sum(msg, seg, num_segments=R * N)
        agg = agg.reshape(R, N, NUM_BASES, SUBMAT_IN)
        W = weight.reshape(R, NUM_BASES, SUBMAT_IN, SUBMAT_OUT)
        out = jnp.einsum('rnbi,rbio->nbo', agg, W)
        return out.reshape(N, NUM_BASES * SUBMAT_OUT)

    def _L0_ffn_ref(x, Wr, br, W1, b1, W2, b2, gamma, beta):
        import math
        import jax, jax.numpy as jnp
        import numpy as np
        CAPACITY_FACTOR = 1.25
        TOP_K = 2
        LN_EPS = 1e-05

        def _layer_norm(x, gamma, beta):
            mu = jnp.mean(x, axis=-1, keepdims=True)
            var = jnp.var(x, axis=-1, keepdims=True)
            return (x - mu) * jax.lax.rsqrt(var + LN_EPS) * gamma + beta
        B, S, D = x.shape
        E = Wr.shape[1]
        N = B * S
        K = TOP_K
        logits = jnp.mean(x, axis=1) @ Wr + br
        routing_weights = jax.nn.softmax(logits, axis=-1)
        capacity = float(math.ceil(N * CAPACITY_FACTOR / E))
        expected_loads = routing_weights.sum(axis=0) * (N / B)
        scale = jnp.where(expected_loads > capacity, capacity / expected_loads, 1.0)
        routing_weights = jax.nn.softmax(routing_weights * scale, axis=-1)
        rw_tok = jnp.broadcast_to(routing_weights[:, None, :], (B, S, E)).reshape(N, E)
        top_w, top_i = jax.lax.top_k(rw_tok, K)
        top_w = jax.nn.softmax(top_w, axis=-1)
        xf = x.reshape(N, D)
        h = jax.nn.gelu(jnp.einsum('nd,edf->enf', xf, W1) + b1[:, None, :], approximate=False)
        y = jnp.einsum('enf,efd->end', h, W2) + b2[:, None, :]
        w_dense = jnp.zeros((N, E), x.dtype).at[jnp.arange(N)[:, None], top_i].add(top_w)
        out = jnp.einsum('ne,end->nd', w_dense, y).reshape(B, S, D)
        out = _layer_norm(out + x, gamma, beta)
        return out

    def _L1_gnn_ref(x, edge_index, W, a_src, a_dst):
        import jax, jax.numpy as jnp
        import numpy as np
        N = 6250
        E = 100000
        IN_C = 256
        HEADS = 8
        OUT_C = 32
        n = x.shape[0]
        H, D = a_src.shape
        x_proj = (x @ W).reshape(n, H, D)
        alpha_src = jnp.einsum('nhd,hd->nh', x_proj, a_src)
        alpha_dst = jnp.einsum('nhd,hd->nh', x_proj, a_dst)
        row, col = (edge_index[0], edge_index[1])
        e = alpha_src[row] + alpha_dst[col]
        m = jax.ops.segment_max(e, col, num_segments=n)
        m = jnp.where(jnp.isfinite(m), m, 0.0)
        e_exp = jnp.exp(e - m[col])
        s = jax.ops.segment_sum(e_exp, col, num_segments=n)
        att = e_exp / (s[col] + 1e-16)
        out = jax.ops.segment_sum(att[:, :, None] * x_proj[row], col, num_segments=n)
        return out.reshape(n, H * D)

    def _L1_ffn_ref(x, Wr, br, W1, b1, g1, be1, m1, v1, W2, b2, g2, be2, m2, v2, Wo, bo):
        import jax, jax.numpy as jnp
        import numpy as np
        BN_EPS = 0.001

        def _bn(h, g, b, m, v):
            return g * (h - m) * jax.lax.rsqrt(v + BN_EPS) + b
        feat = jnp.mean(x, axis=0)
        w = jax.nn.softmax(feat @ Wr + br, axis=-1)
        h = jnp.einsum('bfd,edh->bfeh', x, W1) + b1
        h = jax.nn.relu(_bn(h, g1, be1, m1, v1))
        h = jnp.einsum('bfeh,ehk->bfek', h, W2) + b2
        h = jax.nn.relu(_bn(h, g2, be2, m2, v2))
        y = jnp.einsum('bfeh,ehd->bfed', h, Wo) + bo
        return jnp.einsum('bfed,fe->bfd', y, w)
    edge_index = jnp.stack([src, dst])
    x = x + _L0_gnn_ref(_layernorm(x, axis=-1), L0_gnn_weight, src, dst, edge_type_8, edge_weight)
    x = x + _L0_ffn_ref(_layernorm(x, axis=-1)[None], L0_ffn_Wr, L0_ffn_br, L0_ffn_W1, L0_ffn_b1, L0_ffn_W2, L0_ffn_b2, L0_ffn_gamma, L0_ffn_beta)[0]
    x = x + _L1_gnn_ref(_layernorm(x, axis=-1), edge_index, L1_gnn_W, L1_gnn_a_src, L1_gnn_a_dst)
    x = x + _L1_ffn_ref(_layernorm(x, axis=-1)[None], L1_ffn_Wr, L1_ffn_br, L1_ffn_W1, L1_ffn_b1, L1_ffn_g1, L1_ffn_be1, L1_ffn_m1, L1_ffn_v1, L1_ffn_W2, L1_ffn_b2, L1_ffn_g2, L1_ffn_be2, L1_ffn_m2, L1_ffn_v2, L1_ffn_Wo, L1_ffn_bo)[0]
    return x

_drawn_inputs = setup_inputs


def setup_inputs(seed=0):
    import zlib

    import numpy as np

    out = dict(_drawn_inputs(seed))
    spreads = {'L0_ffn_br': (0.0, 0.8),
     'L0_ffn_b1': (0.0, 0.421),
     'L0_ffn_b2': (0.0, 0.28),
     'L0_ffn_gamma': (1.0, 0.2),
     'L0_ffn_beta': (0.0, 0.1),
     'L1_ffn_br': (0.0, 0.8),
     'L1_ffn_b1': (0.0, 0.705),
     'L1_ffn_g1': (1.0, 0.6),
     'L1_ffn_be1': (0.0, 0.76),
     'L1_ffn_m1': (0.0, 0.724),
     'L1_ffn_v1': (1.0, 0.6),
     'L1_ffn_b2': (0.0, 0.519),
     'L1_ffn_g2': (1.0, 0.6),
     'L1_ffn_be2': (0.0, 0.574),
     'L1_ffn_m2': (0.0, 0.513),
     'L1_ffn_v2': (1.0, 0.6),
     'L1_ffn_bo': (0.0, 0.395)}
    factors = {'L0_ffn_Wr': 8.0, 'L1_gnn_a_dst': 64.0}
    for name, (base, spread) in spreads.items():
        noise = np.random.default_rng([zlib.crc32(name.encode()), seed]).standard_normal(out[name].shape)
        drawn = base * np.exp(spread * noise) if base else spread * noise
        out[name] = jnp.asarray(drawn.astype(out[name].dtype))
    for name, factor in factors.items():
        out[name] = (out[name] * factor).astype(out[name].dtype)
    return out
```

```python
from contextlib import ExitStack

import numpy as np

import concourse.bass as bass
from concourse import mybir

ALU = mybir.AluOpType
ACT = mybir.ActivationFunctionType
AX = mybir.AxisListType.X
F32 = mybir.dt.float32
I32 = mybir.dt.int32

P = 128
N = 6250
D = 256
H = D // P
E = 206250
RELS = 8
HEADS = 8
HD = D // HEADS
EXPERTS = 8
F0 = 512

NODE_TILES = -(-N // P)
NP = NODE_TILES * P
LAST_ROWS = N - (NODE_TILES - 1) * P
GROUP = 4
GCOLS = GROUP * P
GROUPS = NODE_TILES // GROUP
assert NODE_TILES == GROUPS * GROUP + 1

TILES = -(-E // P)
BT = 16
BATCHES = -(-TILES // BT)
LAST_TILES = TILES - (BATCHES - 1) * BT
assert BATCHES % 2 == 1
BLOCKS = -(-TILES // P)
TPAD = BLOCKS * P
PAD_NODE = N
COLS = -(-(N + P) // P) * P

BANK = 512
ROW1 = D + HEADS
BIG = 1.0e38
LN_EPS = 1e-5
BN_EPS = 1e-3
CAPACITY = float(-(-(N * 5) // (4 * EXPERTS)))


class Named:
    pass


def allocator(nc, ctx):
    a = Named()
    a.sb = lambda name, shape, dt=F32: ctx.enter_context(nc.sbuf_tensor(name, shape, dt))
    a.ps = lambda name, shape: ctx.enter_context(nc.psum_tensor(name, shape, F32))

    def bank(name, *shape):
        n = int(np.prod(shape))
        v = a.ps(name, [P, BANK])[:, 0:n]
        return v if len(shape) == 1 else v.rearrange("p (a b) -> p a b", b=shape[-1])
    a.bank = bank
    held = []

    def sem(name):
        held.append(nc.alloc_semaphore(name))
        return held[-1]

    def release():
        if held:
            nc.clear_and_free_semaphores(held)
            nc.all_engine_barrier()
    ctx.callback(release)
    a.sem = sem
    a.sems = lambda name, n: [a.sem(f"{name}{i}") for i in range(n)]
    return a


class Steps:

    def __init__(self, eng, sem, base=0, k=None):
        self.eng, self.sem, self.base, self.n, self.k = eng, sem, base, 0, k

    def done(self, ins):
        ins.then_inc(self.sem, 1)
        self.n += 1

    def wait(self):
        self.eng.wait_ge(self.sem, self.base + self.n)

    def then(self, ins):
        self.done(ins)
        self.wait()


def node_pairs(eng, emit):
    with eng.Fori(0, NODE_TILES // 2) as i:
        emit(i, 0, P)
        emit(i, 1, P)
    emit(NODE_TILES // 2, 0, LAST_ROWS)


def batch_pairs(eng, emit):
    with eng.Fori(0, BATCHES // 2) as i:
        emit(i, 0, BT)
        emit(i, 1, BT)
    emit(BATCHES // 2, 0, LAST_TILES)


def cols(start, n):
    return bass.ds(start, n)


def inverse_root(dve, st, x, guess, t):
    past_waits(dve, st.k)
    st.then(dve.tensor_scalar(t.bitcast(I32), x.bitcast(I32), 1, None, ALU.arith_shift_right))
    st.then(dve.tensor_scalar(guess.bitcast(I32), t.bitcast(I32), -1.0, float(0x5f3759df), ALU.mult, ALU.add))
    for _ in range(3):
        st.then(dve.tensor_tensor(t, guess, guess, ALU.mult))
        st.then(dve.tensor_tensor(t, t, x, ALU.mult))
        st.then(dve.tensor_scalar(t, t, -0.5, 1.5, ALU.mult, ALU.add))
        st.then(dve.tensor_tensor(guess, guess, t, ALU.mult))


INVERSE_ROOT_STEPS = 14


class Norm:
    STEPS, STEPS_ALONE = 3, 4 + INVERSE_ROOT_STEPS

    def __init__(self, a, k, name):
        self.stats, self.mv = a.sb(name + "stats", [P, 6]), a.sb(name + "mv", [P, 2])
        self.rstd, self.tmp = a.sb(name + "rstd", [P, 1]), a.sb(name + "tmp", [P, 1])
        self.asked, self.rooted = a.sem(name + "asked"), a.sem(name + "rooted")
        self.k = k

    def apply(self, dve, st, m, x, out, r):
        past_waits(dve, self.k)
        st.then(dve.bn_stats(self.stats[:r, :], x))
        past_waits(dve, self.k)
        dve.bn_aggr(self.mv[:r, :], self.stats[:r, :]).then_inc(self.asked, 1)
        dve.wait_ge(self.rooted, m + 1)
        st.then(dve.reciprocal(self.rstd[:r, :], self.rstd[:r, :]))
        st.then(dve.tensor_scalar(out, x, self.mv[:r, 0:1], self.rstd[:r, 0:1], ALU.subtract, ALU.mult))

    def root(self, act, m, r):
        act.wait_ge(self.asked, m + 1)
        act.activation(self.rstd[:r, :], self.mv[:r, 1:2], ACT.Sqrt, bias=self.k.eps[:r, :]
                       ).then_inc(self.rooted, 1)

    def apply_alone(self, dve, st, x, out, r):
        past_waits(dve, self.k)
        st.then(dve.bn_stats(self.stats[:r, :], x))
        past_waits(dve, self.k)
        st.then(dve.bn_aggr(self.mv[:r, :], self.stats[:r, :]))
        var = self.mv[:r, 1:2]
        st.then(dve.tensor_scalar(var, var, LN_EPS, None, ALU.add))
        inverse_root(dve, st, var, self.rstd[:r, :], self.tmp[:r, :])
        st.then(dve.tensor_scalar(out, x, self.mv[:r, 0:1], self.rstd[:r, 0:1], ALU.subtract, ALU.mult))


def past_waits(eng, k):
    eng.sem_inc(k.passed, 1)


def constants(nc, k):
    with ExitStack() as ctx:
        a = allocator(nc, ctx)
        diff = a.sb("diff", [P, P], I32)
        column = a.sb("column", [P, P], I32)
        made, s = a.sem("iota_made"), a.sem("const_steps")
        t_ps = a.bank("t_ps", P)
        t_done = a.sem("e8t_turned")
        block = ctx.enter_context(nc.Block())

        @block.gpsimd
        def _(pool):
            pool.iota(diff[:], [[1, P]], base=0, channel_multiplier=-1).then_inc(made, 1)
            pool.iota(column[:], [[1, P]], base=0, channel_multiplier=0).then_inc(made, 1)
            pool.memset(k.acc[:], 0.0).then_inc(made, 1)

        @block.tensor
        def _(pe):
            pe.wait_ge(s, 4)
            pe.transpose(t_ps[0:HEADS, :], k.head_of[:], k.ident[:]).then_inc(t_done, 1)

        @block.vector
        def _(dve):
            st = Steps(dve, s, 0, k)
            dve.wait_ge(made, 2)
            st.then(dve.tensor_scalar(k.ident[:], diff[:], 0.0, None, ALU.is_equal))
            st.then(dve.tensor_copy(k.iota[:], column[:]))
            st.then(dve.tensor_reduce(k.head_of[:], k.ident[:].rearrange("p (h t) -> p h t", h=HEADS),
                                      AX, ALU.add))
            st.then(dve.tensor_reduce(k.tile_of[:], k.ident[:].rearrange("p (h t) -> p t h", h=HEADS),
                                      AX, ALU.add))
            st.done(dve.tensor_copy(k.head_rows[:].rearrange("h (g c) -> h g c", c=HD),
                                    k.ident[0:HEADS, 0:HEADS].unsqueeze(2).broadcast_to([HEADS, HEADS, HD])))
            st.done(dve.memset(k.ones[:], 1.0))
            st.done(dve.memset(k.eps[:], LN_EPS))
            dve.wait_ge(t_done, 1)
            st.done(dve.tensor_copy(k.head_of_t[:], t_ps[0:HEADS, :]))
            dve.wait_ge(made, 3)
            st.wait()


def edge_tables(nc, k, g):
    whole, rest = (TILES // P) * P * P, E % P
    rows = TILES - 1 - (TILES // P) * P
    with ExitStack() as ctx:
        a = allocator(nc, ctx)
        dst_i = a.sb("dst_i", [P, BLOCKS, P], I32)
        src_i = a.sb("src_i", [P, BLOCKS, P], I32)
        rel_i = a.sb("rel_i", [P, BLOCKS, P], I32)
        prev_i = a.sb("prev_i", [P, BLOCKS], I32)
        weight = a.sb("weight", [P, BLOCKS, P])
        row0 = a.sb("row0", [P, BLOCKS, P])
        src_f = a.sb("src_f", [P, BLOCKS, P])
        off_f = a.sb("off_f", [P, BLOCKS, P])
        dst_f = a.sb("dst_f", [P, BLOCKS, P])
        prev_f = a.sb("prev_f", [P, BLOCKS])
        starts = a.sb("starts", [P, BLOCKS, P + 1])
        ends = a.sb("ends", [P, BLOCKS, 2])
        both = a.sb("both", [P, BLOCKS])
        base_c, base_f = a.sb("base_c", [P, BLOCKS], I32), a.sb("base_f", [P, BLOCKS])
        base_row = a.sb("base_row", [P, TPAD])
        far = a.sb("far", [P, 1])
        turned = a.ps("turned", [P, 2, 4, P])
        filled, loaded = a.sem("filled"), a.sem("edges_loaded")
        s, ready = a.sem("edge_steps"), a.sem("edge_arrays")
        turn, taken = a.sem("turned_q"), a.sem("taken_q")
        stored, back = a.sem("edge_stored"), a.sem("edge_back")
        block = ctx.enter_context(nc.Block())

        def flat(ap):
            return ap.rearrange("(k q e) -> q k e", q=P, e=P)

        loads = []
        for name, t in (("dst", dst_i), ("src", src_i), ("edge_type_8", rel_i), ("edge_weight", weight)):
            arr = g[name]
            loads += [(t[:, 0:BLOCKS - 1, :], flat(arr[0:whole])),
                      (t[0:rows, BLOCKS - 1, :], arr[whole:whole + rows * P].rearrange("(q e) -> q e", e=P)),
                      (t[rows:rows + 1, BLOCKS - 1, 0:rest],
                       arr[E - rest:E].rearrange("(q e) -> q e", e=rest))]
        before = g["dst"][0:(TILES - 1) * P].rearrange("(t e) -> t e", e=P)[:, P - 1:P]
        loads += [(prev_i[1:P, 0:1], before[0:P - 1, :])]
        for b in range(1, BLOCKS):
            n = min(P, TILES - b * P)
            loads += [(prev_i[0:n, b:b + 1], before[b * P - 1:b * P - 1 + n, :])]

        @block.gpsimd
        def _(pool):
            pool.memset(k.base[:, 0:BT], 0).then_inc(filled, 1)
            for t, v in ((dst_i, PAD_NODE), (src_i, 0), (rel_i, 0)):
                pool.memset(t[:, BLOCKS - 1, :], v).then_inc(filled, 1)
            pool.memset(weight[:, BLOCKS - 1, :], 0.0).then_inc(filled, 1)
            pool.memset(prev_i[:], PAD_NODE).then_inc(filled, 1)
            pool.memset(starts[:], 0.0).then_inc(filled, 1)
            pool.wait_ge(filled, 7)
            pool.memset(prev_i[0:1, 0:1], -1).then_inc(filled, 1)
            pool.wait_ge(filled, 8)

        @block.sync
        def _(sp):
            sp.wait_ge(filled, 8)
            with nc.allow_non_contiguous_dma(reason="one destination per tile"):
                for dst, src in loads:
                    sp.dma_start(dst, src).then_inc(loaded, 16)
            sp.wait_ge(ready, 1)
            with nc.allow_non_contiguous_dma(reason="one base per tile"):
                for h in range(HEADS):
                    sp.dma_start(k.starts_d[h].rearrange("(k q) e -> q k e", q=P), starts[:]
                                 ).then_inc(stored, 16)
                sp.dma_start(k.ends_d.rearrange("(k q) e -> q k e", q=P), ends[:]).then_inc(stored, 16)
                sp.dma_start(k.both_d.rearrange("(k q) -> q k", q=P), both[:]).then_inc(stored, 16)
                sp.dma_start(k.base_d.rearrange("(k q) -> q k", q=P), base_c[:]).then_inc(stored, 16)
                sp.dma_start(k.base_f_d.rearrange("(k q) -> q k", q=P), base_f[:]).then_inc(stored, 16)
            sp.wait_ge(stored, 16 * (HEADS + 4))
            flat_ends = k.ends_d.rearrange("(a t) e -> a (t e)", a=1)
            sp.dma_start(k.ends8[:], flat_ends.broadcast_to([HEADS, 2 * TPAD])).then_inc(back, 16)
            sp.dma_start(k.both8[:], k.both_d.rearrange("(a t) -> a t", a=1).broadcast_to([HEADS, TPAD])
                         ).then_inc(back, 16)
            sp.dma_start(k.base[:, BT:BT + TPAD], k.base_d.rearrange("(a t) -> a t", a=1)).then_inc(back, 16)
            sp.dma_start(base_row[:], k.base_f_d.rearrange("(a t) -> a t", a=1).broadcast_to([P, TPAD])
                         ).then_inc(back, 16)
            sp.wait_ge(back, 64)

        @block.vector
        def _(dve):
            st = Steps(dve, s, 0, k)
            dve.wait_ge(loaded, 16 * len(loads))
            st.done(dve.tensor_copy(dst_f[:], dst_i[:]))
            st.done(dve.tensor_copy(prev_f[:], prev_i[:]))
            st.done(dve.tensor_copy(base_c[:], dst_i[:, :, 0]))
            st.done(dve.tensor_copy(base_f[:], dst_i[:, :, 0]))
            st.done(dve.scalar_tensor_tensor(row0[:], rel_i[:], float(NP), src_i[:], ALU.mult, ALU.add))
            st.then(dve.tensor_copy(src_f[:], src_i[:]))
            st.done(dve.tensor_tensor(off_f[:], dst_f[:], dst_f[:, :, 0:1].broadcast_to([P, BLOCKS, P]),
                                      ALU.subtract))
            st.done(dve.tensor_tensor(starts[:, :, 1:P], dst_f[:, :, 1:P], dst_f[:, :, 0:P - 1],
                                      ALU.not_equal))
            st.done(dve.tensor_tensor(starts[:, :, 0], dst_f[:, :, 0], prev_f[:], ALU.not_equal))
            st.done(dve.tensor_tensor(ends[:, :, 0], dst_f[:, :, 0], prev_f[:], ALU.not_equal))
            st.then(dve.tensor_tensor(ends[:, :, 1], dst_f[:, :, P - 1], dst_f[:, :, 0], ALU.not_equal))
            st.done(dve.tensor_scalar(starts[:], starts[:], -BIG, None, ALU.mult))
            st.then(dve.tensor_scalar(ends[:], ends[:], -BIG, None, ALU.mult))
            st.then(dve.tensor_tensor(both[:], ends[:, :, 0], ends[:, :, 1], ALU.add))
            dve.sem_inc(ready, 1)
            n = 0
            for kind in range(4):
                for b in range(0, BLOCKS, 4):
                    m = min(4, BLOCKS - b)
                    dve.wait_ge(turn, n + 1)
                    st.then(dve.tensor_copy(k.meta[:, kind, b * P:(b + m) * P],
                                            turned[:, n % 2, 0:m, :].rearrange("p a b -> p (a b)")))
                    dve.sem_inc(taken, 1)
                    n += 1
            dve.wait_ge(back, 64)
            st.then(dve.tensor_tensor(k.near[:], k.meta[:, OFF_KIND, :], base_row[:], ALU.add))
            near = k.near[:].rearrange("p (b t) -> p b t", t=BT)
            first = base_row[:].rearrange("p (b t) -> p b t", t=BT)[:, :, 0:1]
            st.then(dve.tensor_tensor(near, near, first.broadcast_to([P, TPAD // BT, BT]), ALU.subtract))
            st.then(dve.tensor_reduce(far[:], k.near[:], AX, ALU.max))
            dve.sem_inc(taken, 1)
            dve.wait_ge(turn, n + 1)
            st.then(dve.tensor_reduce(far[0:1, :], turned[0:1, 0, 0, :], AX, ALU.max))
            st.then(dve.tensor_scalar(k.narrow[:], far[0:1, :], float(P), None, ALU.is_lt))

        @block.tensor
        def _(pe):
            pe.wait_ge(ready, 1)
            n = 0
            for arr in (row0, src_f, off_f, weight):
                for b in range(0, BLOCKS, 4):
                    m = min(4, BLOCKS - b)
                    if n >= 2:
                        pe.wait_ge(taken, n - 1)
                    for j in range(m):
                        ins = pe.transpose(turned[:, n % 2, j, :], arr[:, b + j, :], k.ident[:])
                    ins.then_inc(turn, 1)
                    n += 1
            pe.wait_ge(taken, n + 1)
            pe.transpose(turned[0:1, 0, 0, :], far[:], k.ident[:]).then_inc(turn, 1)


ROW0_KIND, SRC_KIND, OFF_KIND, WEIGHT_KIND = range(4)


def relation_table(nc, k, g):
    with ExitStack() as ctx:
        a = allocator(nc, ctx)
        x = [a.sb(f"rx{i}", [P, D]) for i in range(2)]
        xn = [a.sb(f"rxn{i}", [P, D]) for i in range(2)]
        xt = [a.sb(f"rxt{i}", [P, H, P]) for i in range(2)]
        rows = [a.sb(f"rrows{i}", [P, RELS, D]) for i in range(2)]
        wblk = a.sb("wblk", [P, H, RELS, P])
        norm_ = Norm(a, k, "r")
        t_ps = a.ps("rt_ps", [P, 2, H, P])
        y_ps = [a.bank(f"ry_ps{i}", 4, P) for i in range(4)]
        wload, zeroed = a.sem("wload"), a.sem("wzeroed")
        xload = a.sems("xload", 2)
        s, normed, turned, taken = a.sem("rsteps"), a.sem("normed"), a.sem("rturned"), a.sem("rtaken")
        made, moved = a.sems("made", 4), a.sems("rmoved", 4)
        xfree, stored = a.sem("xfree"), a.sems("rstored", 2)
        block = ctx.enter_context(nc.Block())
        table = k.table0_d.rearrange("(r n) d -> n r d", r=RELS)
        PER = Norm.STEPS + 1

        @block.gpsimd
        def _(pool):
            pool.memset(wblk[:], 0.0).then_inc(zeroed, 1)
            pool.memset(x[0][:], 0.0).then_inc(zeroed, 1)
            pool.memset(x[1][:], 0.0).then_inc(zeroed, 1)

        @block.sync
        def _(sp):
            sp.wait_ge(zeroed, 3)
            w = g["L0_gnn_weight"].rearrange("r (b i o) -> b i r o", i=32, o=32)
            for b in range(D // 32):
                q = 32 * (b % 4)
                sp.dma_start(wblk[q:q + 32, b // 4, :, q:q + 32], w[b]).then_inc(wload, 16)

            def load(i, par, rows_):
                sp.wait_ge(xfree, 2 * i + par + 1)
                sp.dma_start(x[par][:rows_, :], g["x"][cols((2 * i + par) * P, rows_), :]
                             ).then_inc(xload[par], 16)
            node_pairs(sp, load)

        @block.vector
        def _(dve):
            dve.sem_inc(xfree, 2)
            dve.wait_ge(zeroed, 3)

            def norm(i, par, rows_):
                t = 2 * i + par
                st = Steps(dve, s, PER * t, k)
                dve.wait_ge(xload[par], 16 * (i + 1))
                dve.wait_ge(turned, t + 1)
                norm_.apply(dve, st, t, x[par][:], xn[par][:], P)
                dve.sem_inc(xfree, 1)
                dve.sem_inc(normed, 1)
                dve.wait_ge(turned, t + 3)
                st.then(dve.tensor_copy(xt[par][:], t_ps[:, par, :, :]))
                dve.sem_inc(taken, 1)
                dve.wait_ge(stored[par], 16 * (i + 1))
                for c in (0, 1):
                    dve.wait_ge(made[c], t + 1)
                    dve.tensor_copy(rows[par][:, 4 * (c % 2):4 * (c % 2) + 4, (c // 2) * P:(c // 2 + 1) * P],
                                    y_ps[c]).then_inc(moved[c], 1)
            node_pairs(dve, norm)
            dve.wait_ge(s, PER * NODE_TILES)

        @block.tensor
        def _(pe):
            pe.sem_inc(turned, 2)
            pe.wait_ge(wload, 16 * (D // 32))
            for c in range(4):
                pe.sem_inc(moved[c], 1)

            def mult(i, par, rows_):
                t = 2 * i + par
                pe.wait_ge(normed, t + 1)
                for h in range(H):
                    ins = pe.transpose(t_ps[:, par, h, :], xn[par][:, h * P:(h + 1) * P], k.ident[:])
                ins.then_inc(turned, 1)
                pe.wait_ge(taken, t + 1)
                for h in range(H):
                    for r in range(2):
                        c = 2 * h + r
                        pe.wait_ge(moved[c], t + 1)
                        pe.matmul(y_ps[c].rearrange("p a b -> p (a b)"), xt[par][:, h, :],
                                  wblk[:, h, 4 * r:4 * r + 4, :].rearrange("p a b -> p (a b)"),
                                  start=True, stop=True).then_inc(made[c], 1)
            node_pairs(pe, mult)

        @block.scalar
        def _(act):
            act.sem_inc(stored[0], 16)
            act.sem_inc(stored[1], 16)

            def move(i, par, rows_):
                t = 2 * i + par
                norm_.root(act, t, P)
                act.wait_ge(stored[par], 16 * (i + 1))
                for c in (2, 3):
                    act.wait_ge(made[c], t + 1)
                    act.copy(rows[par][:, 4 * (c % 2):4 * (c % 2) + 4, (c // 2) * P:(c // 2 + 1) * P],
                             y_ps[c]).then_inc(moved[c], 1)
                for c in range(4):
                    act.wait_ge(moved[c], t + 2)
                act.dma_start(table[cols(t * P, P), :, :], rows[par][:]).then_inc(stored[par], 16)
            node_pairs(act, move)
            act.wait_ge(stored[0], 16 * (NODE_TILES // 2 + 2))
            act.wait_ge(stored[1], 16 * (NODE_TILES // 2 + 1))


def gnn0_edges(nc, k):
    with ExitStack() as ctx:
        a = allocator(nc, ctx)
        ring = [a.sb(f"ring0_{i}", [P, D]) for i in range(2 * BT)]
        onehot = [a.sb(f"onehot0_{i}", [P, P]) for i in range(4)]
        index = [a.sb(f"index0_{i}", [P, BT], I32) for i in range(2)]
        scal = [a.sb(f"scal0_{i}", [P, 2, BT]) for i in range(2)]
        win = [a.bank(f"win0_{i}", H, P) for i in range(4)]
        got = k.got0
        hot = a.sems("hot0_", BT)
        used = a.sems("used0_", BT)
        added = a.sems("added0_", BT)
        indexed, staged = a.sem("indexed0_"), a.sem("staged0_")
        block = ctx.enter_context(nc.Block())

        @block.scalar
        def _(act):
            def stage_index(b, par):
                act.copy(index[par][:], k.meta[:, ROW0_KIND, cols(b * BT, BT)]).then_inc(indexed, 1)

            def stage_scal(b, par):
                act.copy(scal[par][:], k.meta[:, OFF_KIND:WEIGHT_KIND + 1, cols(b * BT, BT)]
                         ).then_inc(staged, 1)

            def ahead(i, par):
                b = 2 * i + par
                for t in range(BT):
                    act.wait_ge(got[par * BT + t], 16 * (i + 1))
                stage_index(b + 2, par)
                act.wait_ge(used[BT - 1], b + 3)
                stage_scal(b + 2, par)

            for par in range(2):
                stage_index(par, par)
                stage_scal(par, par)
            with act.Fori(0, BATCHES // 2) as i:
                ahead(i, 0)
                ahead(i, 1)

        @block.gpsimd
        def _(pool):
            def gather(i, par, tiles):
                b = 2 * i + par
                pool.wait_ge(indexed, b + 1)
                for t in range(tiles):
                    pool.wait_ge(used[t], b + 1)
                    past_waits(pool, k)
                    pool.indirect_dma_start(ring[par * BT + t][:], None, k.table0_d,
                                            bass.IndirectOffsetOnAxis(ap=index[par][:, t:t + 1], axis=0)
                                            ).then_inc(got[par * BT + t], 16)
            batch_pairs(pool, gather)

        @block.tensor
        def _(pe):
            for t in range(BT):
                pe.sem_inc(used[t], 2)

            def sums(i, par, tiles):
                b = 2 * i + par
                for t in range(tiles):
                    pe.wait_ge(got[par * BT + t], 16 * (i + 1))
                    pe.wait_ge(hot[t], b + 1)
                    pe.wait_ge(added[(t - 4) % BT], b + 2 if t >= 4 else b + 1)
                    for h in range(H):
                        ins = pe.matmul(win[t % 4][:, h, :], ring[par * BT + t][:, h * P:(h + 1) * P],
                                        onehot[t % 4][:], start=True, stop=True)
                    ins.then_inc(used[t], 1)
            batch_pairs(pe, sums)

        @block.vector
        def _(dve):
            for t in range(BT):
                dve.sem_inc(added[t], 1)

            def tiles_of(i, par, tiles):
                b = 2 * i + par
                dve.wait_ge(staged, b + 1)
                _, bases = nc.values_load_multi_w_load_instructions(
                    k.base[0:1, cols(b * BT + BT, tiles)], engines=[dve.engine], min_val=0, max_val=COLS - P)

                def one_hot(t):
                    dve.wait_ge(used[(t - 4) % BT], b + 3 if t >= 4 else b + 2)
                    dve.tensor_scalar(onehot[t % 4][:], k.iota[:], scal[par][:, 0, t:t + 1],
                                      scal[par][:, 1, t:t + 1], ALU.is_equal, ALU.mult).then_inc(hot[t], 1)

                one_hot(0)
                one_hot(1)
                for t in range(tiles):
                    if t + 2 < tiles:
                        one_hot(t + 2)
                    dve.wait_ge(used[t], b + 3)
                    dve.wait_ge(added[(t - 1) % BT], b + 2 if t else b + 1)
                    sums = k.acc[:, :, cols(bases[t], P)]
                    dve.tensor_tensor(sums, sums, win[t % 4][:], ALU.add).then_inc(added[t], 1)
            batch_pairs(dve, tiles_of)
            dve.wait_ge(added[LAST_TILES - 1], BATCHES + 1)


def gnn0_nodes(nc, k, g):
    with ExitStack() as ctx:
        a = allocator(nc, ctx)
        x = [a.sb(f"nx{i}", [P, D]) for i in range(2)]
        xn = [a.sb(f"nxn{i}", [P, D]) for i in range(2)]
        norm_ = Norm(a, k, "n")
        sums = [a.sb(f"nsums{i}", [P, H, P]) for i in range(2)]
        t_ps = [a.bank(f"nt_ps{i}", H, P) for i in range(2)]
        u_ps = [a.bank(f"nu_ps{i}", H, P) for i in range(2)]
        xload, stored = a.sems("nxload", 2), a.sems("nstored", 2)
        turned, s, normed, back, kept = (a.sem("nturned"), a.sem("nsteps"), a.sem("nnormed"),
                                         a.sem("nback"), a.sem("nkept"))
        fetched = a.sem("nfetched")
        block = ctx.enter_context(nc.Block())
        PER = Norm.STEPS + 1

        @block.sync
        def _(sp):
            sp.sem_inc(stored[0], 16)
            sp.sem_inc(stored[1], 16)

            def io(i, par, rows):
                t = 2 * i + par
                sp.wait_ge(stored[par], 16 * (i + 1))
                sp.dma_start(x[par][:rows, :], g["x"][cols(t * P, rows), :]).then_inc(xload[par], 16)
                sp.wait_ge(s, PER * t + 1)
                sp.dma_start(k.x1_d[cols(t * P, rows), :], x[par][:rows, :]).then_inc(stored[par], 16)
            node_pairs(sp, io)
            sp.wait_ge(stored[0], 16 * (NODE_TILES // 2 + 2))
            sp.wait_ge(stored[1], 16 * (NODE_TILES // 2 + 1))

        @block.tensor
        def _(pe):
            pe.sem_inc(turned, 1)
            pe.sem_inc(back, 2)
            pe.sem_inc(kept, 2 * H)

            def turn(i, par, rows):
                t = 2 * i + par
                pe.wait_ge(fetched, t + 1)
                for h in range(H):
                    ins = pe.transpose(t_ps[par][:rows, h, :], sums[par][:, h, :rows], k.ident[:])
                ins.then_inc(turned, 1)
                pe.wait_ge(normed, t + 1)
                pe.wait_ge(kept, H * t + H)
                for h in range(H):
                    ins = pe.transpose(u_ps[par][:, h, :rows], xn[par][:rows, h * P:(h + 1) * P],
                                       k.ident[:rows, :rows])
                ins.then_inc(back, 1)
            node_pairs(pe, turn)

        @block.vector
        def _(dve):
            def norm(i, par, rows):
                t = 2 * i + par
                st = Steps(dve, s, PER * t, k)
                dve.wait_ge(xload[par], 16 * (i + 1))
                dve.wait_ge(turned, t + 2)
                st.then(dve.tensor_tensor(x[par][:rows, :], x[par][:rows, :],
                                          t_ps[par][:rows].rearrange("p a b -> p (a b)"), ALU.add))
                dve.wait_ge(back, t + 1)
                norm_.apply(dve, st, t, x[par][:rows, :], xn[par][:rows, :], rows)
                dve.sem_inc(normed, 1)
            node_pairs(dve, norm)

        @block.scalar
        def _(act):
            def fetch(t, par, rows):
                act.copy(sums[par][:, :, :rows], k.acc[:, :, cols(t * P, rows)]).then_inc(fetched, 1)

            def keep(i, par, rows):
                t = 2 * i + par
                if rows == P:
                    act.wait_ge(turned, t + 1)
                    fetch(t + 1, 1 - par, P)
                norm_.root(act, t, rows)
                act.wait_ge(back, t + 3)
                for h in range(H):
                    act.activation(k.acc[:, h, cols(t * P, rows)], u_ps[par][:, h, :rows], ACT.Copy,
                                   accum_out=k.node_sums[:, h, cols(t, 1)]).then_inc(kept, 1)
            fetch(0, 0, P)
            node_pairs(act, keep)
            act.wait_ge(kept, H * (NODE_TILES + 2))


def route(nc, k, g):
    X = EXPERTS
    with ExitStack() as ctx:
        a = allocator(nc, ctx)
        mean = a.sb("mean", [P, H])
        wr = a.sb("wr0", [P, H, X])
        br = a.sb("br0", [1, X])
        low_i = a.sb("low_i", [1, X, X], I32)
        low = a.sb("low", [1, X, X])
        num = a.sb("num", [1, X])
        v = [a.sb(f"v{i}", [1, X]) for i in range(8)]
        one = [a.sb(f"one{i}", [1, 1]) for i in range(8)]
        m = [a.sb(f"m{i}", [1, X, X]) for i in range(3)]
        top = a.sb("top", [1, 2])
        pick = a.sb("pick", [1, 2])
        pick_i = a.sb("pick_i", [1, 2], I32)
        tw = a.sb("tw", [1, 2])
        bcast = a.sb("bcast", [P, 2])
        b2 = a.sb("b2_2", [1, 2, D])
        b2s = a.sb("b2s", [1, 2, D])
        lg_ps = a.bank("lg_ps", X)
        w_ps = a.bank("w_ps", 2)
        small, made, s, to_pe, pe_done, to_act, act_done, picked, wload = (
            a.sem(f"route_{n}") for n in ("small", "made", "s", "to_pe", "pe", "to_act", "act", "picked", "w"))
        block = ctx.enter_context(nc.Block())

        @block.gpsimd
        def _(pool):
            pool.iota(low_i[:], [[1, X], [-1, X]], base=0, channel_multiplier=0).then_inc(made, 1)

        @block.sync
        def _(sp):
            sp.dma_start(wr[:], g["L0_ffn_Wr"].rearrange("(h p) x -> p h x", p=P)).then_inc(small, 16)
            sp.dma_start(br[:], g["L0_ffn_br"].rearrange("(a x) -> a x", a=1)).then_inc(small, 16)
            sp.wait_ge(picked, 1)
            _, which = nc.values_load_multi_w_load_instructions(
                pick_i[0:1, 0:2], engines=[sp.engine], min_val=0, max_val=X - 1)
            with nc.allow_non_contiguous_dma(reason="biases onto partitions"):
                for j in range(2):
                    sp.dma_start(k.w1[:, j, :, :], g["L0_ffn_W1"][cols(which[j], 1), :, :].rearrange(
                        "x (h p) f -> p (x h) f", p=P)).then_inc(wload, 16)
                    sp.dma_start(k.w2[:, j, :, :], g["L0_ffn_W2"][cols(which[j], 1), :, :].rearrange(
                        "x (c p) d -> p (x c) d", p=P)).then_inc(wload, 16)
                    sp.dma_start(k.b1[:, j, :], g["L0_ffn_b1"][cols(which[j], 1), :].rearrange(
                        "x (c p) -> p (x c)", p=P)).then_inc(wload, 16)
                    sp.dma_start(b2[:, j, :], g["L0_ffn_b2"][cols(which[j], 1), :]).then_inc(wload, 16)
            sp.wait_ge(wload, 128)

        @block.tensor
        def _(pe):
            pe.wait_ge(small, 32)
            pe.wait_ge(to_pe, 1)
            for h in range(H):
                ins = pe.matmul(lg_ps[0:1, :], mean[:, h:h + 1], wr[:, h, :], start=(h == 0), stop=(h == H - 1))
            ins.then_inc(pe_done, 1)
            pe.wait_ge(to_pe, 2)
            pe.matmul(w_ps, k.ones[0:1, :], tw[:], start=True, stop=True).then_inc(pe_done, 1)

        @block.scalar
        def _(act):
            act.wait_ge(to_act, 1)
            act.activation(v[1][:], v[0][:], ACT.Exp, bias=one[0][:], accum_out=one[1][:]).then_inc(act_done, 1)
            act.wait_ge(to_act, 2)
            act.activation(v[6][:], v[5][:], ACT.Exp, bias=one[3][:], accum_out=one[4][:]).then_inc(act_done, 1)
            act.wait_ge(to_act, 3)
            act.activation(one[6][:], one[5][:], ACT.Exp).then_inc(act_done, 1)

        @block.vector
        def _(dve):
            st = Steps(dve, s, 0, k)
            dve.wait_ge(made, 1)
            st.then(dve.tensor_copy(low[:], low_i[:]))
            st.then(dve.tensor_copy(num[:], low[:, :, 0]))
            st.then(dve.tensor_scalar(low[:], low[:], 0.0, None, ALU.is_gt))
            st.then(dve.tensor_reduce(mean[:], k.node_sums[:], AX, ALU.add))
            st.then(dve.tensor_scalar(mean[:], mean[:], 1.0 / N, None, ALU.mult))
            dve.sem_inc(to_pe, 1)
            dve.wait_ge(pe_done, 1)
            st.then(dve.tensor_tensor(v[0][:], lg_ps[0:1, :], br[:], ALU.add))
            st.then(dve.tensor_reduce(one[0][:], v[0][:], AX, ALU.max, negate=True))
            dve.sem_inc(to_act, 1)
            dve.wait_ge(act_done, 1)
            st.then(dve.reciprocal(one[1][:], one[1][:]))
            st.then(dve.tensor_scalar(v[2][:], v[1][:], one[1][:], None, ALU.mult))
            st.then(dve.tensor_scalar(v[3][:], v[2][:], float(N), 1e-30, ALU.mult, ALU.max))
            st.then(dve.reciprocal(v[4][:], v[3][:]))
            st.then(dve.tensor_scalar(v[4][:], v[4][:], CAPACITY, 1.0, ALU.mult, ALU.min))
            st.then(dve.tensor_tensor(v[5][:], v[2][:], v[4][:], ALU.mult))
            st.then(dve.tensor_reduce(one[3][:], v[5][:], AX, ALU.max, negate=True))
            dve.sem_inc(to_act, 1)
            dve.wait_ge(act_done, 2)
            st.then(dve.reciprocal(one[4][:], one[4][:]))
            st.then(dve.tensor_scalar(v[6][:], v[6][:], one[4][:], None, ALU.mult))
            zi = v[6][:].unsqueeze(2).broadcast_to([1, X, X])
            zj = v[6][:].unsqueeze(1).broadcast_to([1, X, X])
            st.done(dve.tensor_tensor(m[0][:], zj, zi, ALU.is_gt))
            st.then(dve.tensor_tensor(m[1][:], zj, zi, ALU.is_equal))
            st.then(dve.tensor_tensor(m[1][:], m[1][:], low[:], ALU.mult))
            st.then(dve.tensor_tensor(m[0][:], m[0][:], m[1][:], ALU.add))
            st.then(dve.tensor_reduce(v[7][:], m[0][:], AX, ALU.add))
            for j in range(2):
                st.then(dve.tensor_scalar(v[0][:], v[7][:], float(j), None, ALU.is_equal))
                st.then(dve.tensor_tensor(v[1][:], v[0][:], num[:], ALU.mult))
                st.then(dve.tensor_reduce(pick[:, j:j + 1], v[1][:], AX, ALU.add))
                st.then(dve.tensor_tensor(v[1][:], v[0][:], v[6][:], ALU.mult))
                st.then(dve.tensor_reduce(top[:, j:j + 1], v[1][:], AX, ALU.add))
            st.then(dve.tensor_copy(pick_i[:], pick[:]))
            dve.sem_inc(picked, 1)
            st.then(dve.tensor_tensor(one[5][:], top[:, 1:2], top[:, 0:1], ALU.subtract))
            dve.sem_inc(to_act, 1)
            dve.wait_ge(act_done, 3)
            st.then(dve.tensor_scalar(one[7][:], one[6][:], 1.0, None, ALU.add))
            st.then(dve.reciprocal(tw[:, 0:1], one[7][:]))
            st.then(dve.tensor_tensor(tw[:, 1:2], one[6][:], tw[:, 0:1], ALU.mult))
            dve.sem_inc(to_pe, 1)
            dve.wait_ge(pe_done, 2)
            st.then(dve.tensor_copy(bcast[:], w_ps))
            dve.wait_ge(wload, 128)
            for j in range(2):
                st.done(dve.tensor_scalar(k.w2[:, j, :, :], k.w2[:, j, :, :], bcast[:, j:j + 1], None, ALU.mult))
                st.done(dve.tensor_scalar(b2s[:, j, :], b2[:, j, :], tw[:, j:j + 1], None, ALU.mult))
            st.wait()
            st.then(dve.tensor_tensor(k.b2[:], b2s[:, 0, :], b2s[:, 1, :], ALU.add))


def tiles(gi):
    return [LAST_ROWS] if isinstance(gi, int) and gi == GROUPS else [P] * GROUP


def groups(eng, emit, first=0, last=GROUPS - 1):
    with eng.Fori(first, last + 1) as i:
        emit(i)


def ffn0(nc, k, g):
    C = 2 * F0 // P
    with ExitStack() as ctx:
        a = allocator(nc, ctx)
        hid = a.sb("hid", [P, C, GCOLS])
        xg = a.sb("xg", [P, H, GCOLS])
        x1 = a.sb("fx1", [P, GROUP, D])
        y = a.sb("fy", [P, D])
        xn2 = a.sb("fxn2", [P, GROUP, D])
        xt = a.sb("fxt", [P, H, P])
        row = a.sb("frow", [P, 2, ROW1])
        prod = a.sb("fprod", [P, D])
        gamma, beta, asrc = (a.sb(n, [P, D]) for n in ("gamma", "beta", "asrc"))
        wp = a.sb("wp", [P, H, D])
        norm_ = Norm(a, k, "f")
        h_ps = [a.bank(f"fh_ps{i}", GCOLS) for i in range(2)]
        y_ps = [a.bank(f"fy_ps{i}", D) for i in range(2)]
        t_ps = a.bank("ft_ps", H, P)
        p_ps = a.bank("fp_ps", D)
        small = a.sem("fsmall")
        h_made, h_kept = a.sem("h_made"), a.sem("h_kept")
        y_made, y_taken = a.sem("y_made"), a.sem("y_taken")
        x_load = a.sem("fx_load")
        s, normed, x2_done = a.sem("fsteps"), a.sem("fnormed"), a.sem("x2_done")
        x2_stored = a.sem("x2_stored")
        turned, t_kept, p_made, row_done = a.sem("fturned"), a.sem("ft_kept"), a.sem("p_made"), a.sem("row_done")
        row_stored = a.sems("row_stored", 2)
        xg_made = a.sem("xg_made")
        row_steps, p_free = a.sem("row_steps"), a.sem("p_free")
        block = ctx.enter_context(nc.Block())

        def interleaved(head, before, main, after, eng):
            def turn(gi, mine, tail):
                if head and mine:
                    head(gi)
                for t in range(max(len(mine), len(tail))):
                    for f in before if t < len(tail) else ():
                        f(gi - 1, t, tail[t])
                    if t < len(mine):
                        main(gi, t, mine[t])
                    for f in after if t < len(tail) else ():
                        f(gi - 1, t, tail[t])
            turn(0, tiles(0), [])
            groups(eng, lambda gi: turn(gi, tiles(gi), tiles(gi - 1)), 1)
            turn(GROUPS, tiles(GROUPS), [P] * GROUP)
            turn(GROUPS + 1, [], tiles(GROUPS))

        @block.sync
        def _(sp):
            for t, name in ((gamma, "L0_ffn_gamma"), (beta, "L0_ffn_beta")):
                sp.dma_start(t[:], g[name].rearrange("(a d) -> a d", a=1).broadcast_to([P, D])).then_inc(small, 16)
            sp.dma_start(asrc[:], g["L1_gnn_a_src"].rearrange("(a h) d -> a (h d)", a=1).broadcast_to([P, D])
                         ).then_inc(small, 16)
            sp.dma_start(wp[:], g["L1_gnn_W"].rearrange("(h p) d -> p h d", p=P)).then_inc(small, 16)
            sp.sem_inc(x2_stored, 16)
            sp.sem_inc(row_stored[0], 16)
            sp.sem_inc(row_stored[1], 16)

            def rows_of(dram, gi, sizes):
                if len(sizes) == GROUP:
                    return dram[cols(gi * GCOLS, GCOLS), :].rearrange("(t p) d -> p t d", p=P), x1[:]
                return dram[gi * GCOLS:N, :], x1[:sizes[0], 0, :]

            def load(gi):
                sp.wait_ge(x2_stored, 16 * gi + 16)
                if not (isinstance(gi, int) and gi == 0):
                    past_waits(sp, k)
                    sp.wait_ge(normed, GROUP * gi)
                src, dst = rows_of(k.x1_d, gi, tiles(gi))
                sp.dma_start(dst, src).then_inc(x_load, 16)

            def store_x2(gi, t, r):
                if t < len(tiles(gi)) - 1:
                    return
                sp.wait_ge(x2_done, GROUP * gi + t + 1)
                dst, src = rows_of(k.x2_d, gi, tiles(gi))
                sp.dma_start(dst, src).then_inc(x2_stored, 16)

            def store_row(gi, t, r):
                n = GROUP * gi + t
                sp.wait_ge(row_done, n + 1)
                sp.dma_start(k.table1_d[cols(n * P, r), :], row[:r, t % 2, :]).then_inc(row_stored[t % 2], 16)

            interleaved(load, (store_row,), store_x2, (), sp)
            sp.wait_ge(x2_stored, 16 * (GROUPS + 2))
            sp.wait_ge(row_stored[0], 16 * (2 * GROUPS + 2))
            sp.wait_ge(row_stored[1], 16 * (2 * GROUPS + 1))

        @block.tensor
        def _(pe):
            pe.wait_ge(small, 64)
            pe.sem_inc(h_kept, 2)
            pe.sem_inc(p_free, 1)
            pe.sem_inc(y_taken, 2)

            def hidden(gi):
                n = sum(tiles(gi))
                for c in range(C):
                    j, f = c // (C // 2), c % (C // 2)
                    pe.wait_ge(h_kept, C * gi + c + 1)
                    for h in range(H):
                        rhs = k.acc[:, h, cols(gi * GCOLS, n)]
                        ins = pe.matmul(h_ps[c % 2][:, :n], k.w1[:, j, h, f * P:(f + 1) * P], rhs,
                                        start=(h == 0), stop=(h == H - 1))
                    ins.then_inc(h_made, 1)

            def output(gi, t, r):
                pe.wait_ge(y_taken, GROUP * gi + t + 1)
                yb = y_ps[t % 2]
                if t == 0:
                    pe.wait_ge(xg_made, gi + 1)
                for h in range(H):
                    pe.matmul(yb[:r, h * P:(h + 1) * P], xg[:, h, t * P:t * P + r], k.ident[:],
                              start=(h == 0), stop=False, skip_group_check=True)
                pe.matmul(yb[:r, 0:D], k.ones[0:1, 0:r], k.b2[:], start=False, stop=False,
                          skip_group_check=True)
                for c in range(C):
                    if t == 0:
                        pe.wait_ge(h_kept, C * gi + c + 3)
                    ins = pe.matmul(yb[:r, 0:D], hid[:, c, t * P:t * P + r], k.w2[:, c // 4, c % 4, :],
                                    start=False, stop=(c == C - 1), skip_group_check=True)
                ins.then_inc(y_made, 1)

            def turn_back(gi, t, r):
                pe.wait_ge(normed, GROUP * gi + t + 1)
                for h in range(H):
                    ins = pe.transpose(t_ps[:, h, :r], xn2[:r, t, h * P:(h + 1) * P], k.ident[:r, :r])
                ins.then_inc(turned, 1)

            def project(gi, t, r):
                pe.wait_ge(t_kept, GROUP * gi + t + 1)
                pe.wait_ge(p_free, GROUP * gi + t + 1)
                for h in range(H):
                    ins = pe.matmul(p_ps[:r, 0:D], xt[:, h, :r], wp[:, h, :], start=(h == 0), stop=(h == H - 1))
                ins.then_inc(p_made, 1)

            interleaved(hidden, (turn_back,), output, (project,), pe)

        @block.scalar
        def _(act):
            def keep(gi):
                n = sum(tiles(gi))
                for c in range(C):
                    act.wait_ge(h_made, C * gi + c + 1)
                    if c == 0:
                        if not (isinstance(gi, int) and gi == 0):
                            act.wait_ge(y_made, GROUP * gi)
                        act.copy(xg[:, :, :n], k.acc[:, :, cols(gi * GCOLS, n)]).then_inc(xg_made, 1)
                    act.activation(hid[:, c, :n], h_ps[c % 2][:, :n], ACT.Gelu,
                                   bias=k.b1[:, c // 4, c % 4:c % 4 + 1]).then_inc(h_kept, 1)
            keep(0)
            groups(act, keep, 1)
            keep(GROUPS)

        @block.vector
        def _(dve):
            dve.wait_ge(small, 64)
            NPER, RPER = 2 * Norm.STEPS_ALONE + 3, 4

            def norms(gi, t, r):
                n = GROUP * gi + t
                st = Steps(dve, s, NPER * n, k)
                yb = y_ps[t % 2]
                dve.wait_ge(y_made, n + 1)
                if t == 0:
                    dve.wait_ge(x_load, 16 * gi + 16)
                norm_.apply_alone(dve, st, yb[:r, 0:D], y[:r, :], r)
                dve.sem_inc(y_taken, 1)
                st.then(dve.tensor_tensor(y[:r, :], y[:r, :], gamma[:r, :], ALU.mult))
                st.then(dve.tensor_tensor(y[:r, :], y[:r, :], beta[:r, :], ALU.add))
                st.then(dve.tensor_tensor(x1[:r, t, :], x1[:r, t, :], y[:r, :], ALU.add))
                dve.sem_inc(x2_done, 1)
                norm_.apply_alone(dve, st, x1[:r, t, :], xn2[:r, t, :], r)
                assert st.n == NPER
                dve.sem_inc(normed, 1)

            def keep_turned(gi, t, r):
                n = GROUP * gi + t
                dve.wait_ge(turned, n + 1)
                st = Steps(dve, row_steps, RPER * n, k)
                st.then(dve.tensor_copy(xt[:, :, :r], t_ps[:, 0:H, :r]))
                dve.sem_inc(t_kept, 1)

            def make_row(gi, t, r):
                n = GROUP * gi + t
                st = Steps(dve, row_steps, RPER * n + 1, k)
                dve.wait_ge(p_made, n + 1)
                dve.wait_ge(row_stored[t % 2], 16 * (2 * gi + t // 2 + 1))
                st.done(dve.tensor_copy(row[:r, t % 2, 0:D], p_ps[:r, 0:D]))
                st.then(dve.tensor_tensor(prod[:r, :], p_ps[:r, 0:D], asrc[:r, :], ALU.mult))
                dve.sem_inc(p_free, 1)
                st.then(dve.tensor_reduce(row[:r, t % 2, D:ROW1], prod[:r, :].rearrange(
                    "p (h d) -> p h d", h=HEADS), AX, ALU.add))
                assert st.n == RPER - 1
                dve.sem_inc(row_done, 1)

            interleaved(None, (keep_turned,), norms, (make_row,), dve)


def gnn1_edges(nc, k):
    with ExitStack() as ctx:
        a = allocator(nc, ctx)
        ring = a.sb("ring1", [P, 2 * BT, ROW1])
        onehot = a.sb("onehot1", [P, 2, BT, P])
        index = [a.sb(f"index1_{i}", [P, BT], I32) for i in range(2)]
        off = [a.sb(f"off1_{i}", [P, BT]) for i in range(2)]
        starts = [a.sb(f"starts1_{i}", [P, P + 1]) for i in range(2)]
        alpha = a.sb("alpha", [P, BT * HEADS])
        local = a.sb("local", [P, 2 * P])
        spread = a.sb("spread", [P, 2, BT])
        chain = a.sb("chain", [HEADS, 2 * BT + 1])
        joined, ends = a.sb("joined", [HEADS, 2 * BT + 1]), a.sb("ends1", [HEADS, 2 * BT + 1])
        picked = a.sb("picked", [P, 2, BT])
        edge_max = a.sb("edge_max", [P, 2])
        m1, m2 = a.sb("max_forth", [P, P]), a.sb("max_back", [P, P])
        prob = a.sb("prob", [P, BT * HEADS])
        gap, fade = a.sb("gap", [HEADS, 1]), a.sb("fade", [HEADS, 1])
        nodes = a.sb("nodes", [P, ROW1])
        win = [a.bank(f"win1_{i}", 3, P) for i in range(4)]
        batch_win, win_turned = win[0].rearrange("p a b -> p (a b)")[:, 0:ROW1], win[1]
        a_ps, small_ps, p_ps = a.bank("a_ps", P), a.bank("small_ps", 2, P), a.bank("p_ps", P)
        fade_ps = a.bank("fade_ps", H)
        got = k.got1
        hot = a.sems("hot1_", BT)
        used = a.sems("used1_", BT)
        added = a.sems("added1_", BT)
        indexed, staged = a.sem("indexed1_"), a.sem("staged1_")
        st_load, zeroed = a.sems("st_load", 2), a.sem("zeroed1")
        weighted, moved, turned_back = a.sem("g1_weighted"), a.sem("g1_moved"), a.sem("g1_turned_back")
        alpha_c, a_turned, s, to_pe, pe_small, p_turned, p_done, gap_made, fade_made = (
            a.sem(f"g1_{n}") for n in ("alpha", "aturn", "steps", "to_pe", "pe_small", "pturn", "pdone", "gap", "fade"))
        block = ctx.enter_context(nc.Block())
        QUAD = 4

        assert LAST_TILES % QUAD == 0 and LAST_TILES < BT

        def either(eng, narrow, general):
            _, flag = nc.values_load_multi_w_load_instructions(k.narrow[:], engines=[eng.engine],
                                                               min_val=0, max_val=1)
            with eng.If(flag[0] == 1):
                batch_pairs(eng, narrow)
            with eng.Else():
                batch_pairs(eng, general)

        @block.sync
        def _(sp):
            def load(i, par, tiles):
                b = 2 * i + par
                sp.wait_ge(p_done, b + 1)
                sp.dma_start(starts[par][:], k.starts_d[:, cols(b * BT, BT), :]).then_inc(st_load[par], 16)
            batch_pairs(sp, load)

        @block.gpsimd
        def _(pool):
            def gather(i, par, tiles):
                b = 2 * i + par
                pool.wait_ge(indexed, b + 1)
                for t in range(tiles):
                    pool.wait_ge(used[t], b + 1)
                    past_waits(pool, k)
                    pool.indirect_dma_start(ring[:, par * BT + t, :], None, k.table1_d,
                                            bass.IndirectOffsetOnAxis(ap=index[par][:, t:t + 1], axis=0)
                                            ).then_inc(got[par * BT + t], 16)
            batch_pairs(pool, gather)

        @block.scalar
        def _(act):
            act.sem_inc(p_done, 2)
            act.wait_ge(zeroed, 5)
            act.activation(fade[:], k.eps[0:HEADS, :], ACT.Exp)

            def stage_index(b, par):
                act.copy(index[par][:], k.meta[:, SRC_KIND, cols(b * BT, BT)]).then_inc(indexed, 1)

            def stage_off(b, par):
                act.copy(off[par][:], k.meta[:, OFF_KIND, cols(b * BT, BT)]).then_inc(staged, 1)

            def scores(i, par, tiles, between=lambda: None):
                b = 2 * i + par
                for t in range(tiles):
                    act.wait_ge(got[par * BT + t], 16 * (i + 1))
                act.wait_ge(a_turned, b + 1)
                act.copy(alpha[:].rearrange("p (h t) -> p t h", h=HEADS),
                         ring[:, par * BT:(par + 1) * BT, D:ROW1]).then_inc(alpha_c, 1)
                if tiles == BT:
                    stage_index(b + 2, par)
                between()
                act.wait_ge(gap_made, b + 1)
                act.activation(fade[:], gap[:], ACT.Exp).then_inc(fade_made, 1)
                act.wait_ge(p_turned, b + 1)

            def move_window(m, last_tile):
                act.wait_ge(used[last_tile], m + 2)
                act.copy(nodes[:], batch_win).then_inc(moved, 1)

            def narrow(i, par, tiles):
                b = 2 * i + par
                scores(i, par, tiles, lambda: move_window(b, BT - 1))
                act.activation(ring[:, par * BT:(par + 1) * BT, D:ROW1], p_ps.rearrange(
                    "p (h t) -> p t h", h=HEADS), ACT.Exp).then_inc(p_done, 1)
                if tiles == LAST_TILES:
                    move_window(b + 1, LAST_TILES - 1)

            def general(i, par, tiles):
                b = 2 * i + par
                scores(i, par, tiles)
                act.wait_ge(used[BT - 1], b + 2)
                act.activation(prob[:], p_ps, ACT.Exp).then_inc(p_done, 1)
                if tiles == BT:
                    if par == 0:
                        act.wait_ge(used[BT - 1], b + 2)
                    stage_off(b + 1, 1 - par)

            stage_index(0, 0)
            stage_index(1, 1)
            stage_off(0, 0)
            either(act, narrow, general)

        @block.tensor
        def _(pe):
            for t in range(BT):
                pe.sem_inc(used[t], 2)
            pe.sem_inc(a_turned, 1)

            def scores(b, between=lambda: None):
                pe.wait_ge(alpha_c, b + 1)
                pe.wait_ge(p_done, b + 2)
                pe.transpose(a_ps, alpha[:], k.ident[:]).then_inc(a_turned, 1)
                between()
                pe.wait_ge(to_pe, 3 * b + 1)
                pe.matmul(small_ps[0:HEADS, 0, 0:2 * BT], k.head_of[:], spread[:].rearrange("p a b -> p (a b)"),
                          start=True, stop=True).then_inc(pe_small, 1)
                pe.wait_ge(to_pe, 3 * b + 2)
                pe.matmul(small_ps[:, 1, 0:2 * BT + 1], k.head_of_t[:], joined[:], start=True, stop=True
                          ).then_inc(pe_small, 1)
                pe.wait_ge(to_pe, 3 * b + 3)
                pe.transpose(p_ps, m1[:], k.ident[:]).then_inc(p_turned, 1)
                pe.wait_ge(fade_made, b + 1)
                for h in range(H):
                    ins = pe.matmul(fade_ps[:, h:h + 1], k.head_rows[:, h * P:(h + 1) * P], fade[:],
                                    start=True, stop=True)
                ins.then_inc(pe_small, 1)

            def turn_back(m):
                pe.wait_ge(moved, m + 1)
                for h in range(H):
                    pe.transpose(win_turned[:, h, :], nodes[:, h * P:(h + 1) * P], k.ident[:])
                pe.transpose(win_turned[0:HEADS, 2, :], nodes[:, D:ROW1], k.ident[:]).then_inc(turned_back, 1)

            def narrow(i, par, tiles):
                b = 2 * i + par
                scores(b, lambda: turn_back(b))
                for t in range(tiles):
                    if t % QUAD == 0:
                        pe.wait_ge(weighted, BT // QUAD * b + t // QUAD + 1)
                    pe.matmul(batch_win, onehot[:, par, t, :], ring[:, par * BT + t, :],
                              start=(t == 0), stop=(t == tiles - 1)).then_inc(used[t], 1)
                if tiles == LAST_TILES:
                    turn_back(b + 1)

            def general(i, par, tiles):
                b = 2 * i + par
                scores(b)
                for t in range(tiles):
                    pe.wait_ge(hot[t], 2 * b + 2)
                    pe.wait_ge(added[(t - 4) % BT], b + 2 if t >= 4 else b + 1)
                    slot, hot_t = ring[:, par * BT + t, :], onehot[:, 0, t % 4, :]
                    for h in range(H):
                        pe.matmul(win[t % 4][:, h, :], slot[:, h * P:(h + 1) * P], hot_t,
                                  start=True, stop=True)
                    pe.matmul(win[t % 4][0:HEADS, 2, :], prob[:, t:BT * HEADS:BT], hot_t,
                              start=True, stop=True).then_inc(used[t], 1)
            either(pe, narrow, general)

        @block.vector
        def _(dve):
            for t in range(BT):
                dve.sem_inc(added[t], 1)
            st0 = Steps(dve, zeroed, 0, k)
            st0.done(dve.memset(chain[:], -BIG))
            st0.then(dve.memset(k.acc_s[:], 0.0))
            st0.done(dve.memset(k.acc[:, 0, :], 0.0))
            st0.then(dve.memset(k.acc[:, 1, :], 0.0))
            st0.then(dve.memset(batch_win, 0.0))
            SCORES = 15
            FADES = 2

            def scores(b, i, par, st, between=lambda: None):
                before = st.n
                fl = starts[par]
                st.done(dve.tensor_copy(ends[:], k.ends8[:, cols(2 * BT * b, 2 * BT + 1)]))
                dve.wait_ge(a_turned, b + 2)
                dve.wait_ge(st_load[par], 16 * (i + 1))
                st.then(dve.tensor_tensor_scan(local[:, 0:P], fl[:, 0:P], a_ps, -BIG, ALU.add, ALU.max))
                st.then(dve.tensor_tensor_scan(local[:, P:2 * P][:, ::-1], fl[:, 1:P + 1][:, ::-1],
                                               local[:, 0:P][:, ::-1], -BIG, ALU.add, ALU.max))
                st.then(dve.tensor_tensor(spread[:], k.tile_of[:].unsqueeze(1).broadcast_to([P, 2, BT]),
                                          local[:, P - 1:P + 1].unsqueeze(2).broadcast_to([P, 2, BT]), ALU.mult))
                dve.sem_inc(to_pe, 1)
                between()
                dve.wait_ge(pe_small, 3 * b + 1)
                lastfirst = small_ps[0:HEADS, 0, 0:2 * BT]
                st.done(dve.tensor_tensor_scan(chain[:, 2:2 * BT + 1:2], k.both8[:, cols(BT * b, BT)],
                                               lastfirst[:, 0:BT], chain[:, 0:1], ALU.add, ALU.max))
                st.then(dve.tensor_copy(chain[:, 1:2 * BT:2], lastfirst[:, BT:2 * BT]))
                st.then(dve.tensor_tensor_scan(joined[:, ::-1], ends[:, ::-1], chain[:, ::-1], -BIG,
                                               ALU.add, ALU.max))
                dve.sem_inc(to_pe, 1)
                st.then(dve.tensor_tensor(gap[:], chain[:, 0:1], joined[:, 0:1], ALU.subtract))
                dve.sem_inc(gap_made, 1)
                st.then(dve.tensor_copy(chain[:, 0:1], chain[:, 2 * BT:2 * BT + 1]))
                dve.wait_ge(pe_small, 3 * b + 2)
                for j in range(2):
                    st.done(dve.tensor_tensor(picked[:, j, :], small_ps[:, 1, 2 * j:2 * (BT + j) - 1:2],
                                              k.tile_of[:], ALU.mult))
                st.wait()
                st.then(dve.tensor_reduce(edge_max[:], picked[:], AX, ALU.add))
                st.then(dve.tensor_tensor_scan(m1[:], fl[:, 0:P], local[:, P:2 * P], edge_max[:, 0:1],
                                               ALU.add, ALU.max))
                st.then(dve.tensor_tensor_scan(m2[:, ::-1], fl[:, 1:P + 1][:, ::-1], m1[:, ::-1],
                                               edge_max[:, 1:2], ALU.add, ALU.max))
                st.then(dve.tensor_tensor(m1[:], a_ps, m2[:], ALU.subtract))
                dve.sem_inc(to_pe, 1)
                assert st.n - before in (SCORES, SCORES + 2)

            def fade_open(b, base, st):
                dve.wait_ge(pe_small, 3 * b + 3)
                one, one_s = k.acc[:, :, cols(base, 1)], k.acc_s[:, cols(base, 1)]
                st.done(dve.tensor_tensor(one, one, fade_ps.unsqueeze(2), ALU.mult))
                st.then(dve.tensor_tensor(one_s, one_s, fade[:], ALU.mult))

            def base_of(m):
                _, base = nc.values_load_multi_w_load_instructions(
                    k.base[0:1, cols(m * BT, 1)], engines=[dve.engine], min_val=0, max_val=COLS - P)
                return base[0]

            def add_window(m, base, st):
                dve.wait_ge(turned_back, m + 1)
                sums, sums_s = k.acc[:, :, cols(base, P)], k.acc_s[:, cols(base, P)]
                st.done(dve.tensor_tensor(sums, sums, win_turned[:, 0:H, :], ALU.add))
                st.then(dve.tensor_tensor(sums_s, sums_s, win_turned[0:HEADS, 2, :], ALU.add))

            def narrow(i, par, tiles):
                b = 2 * i + par
                st = Steps(dve, s, (SCORES + FADES + 3) * b, k)
                past_waits(dve, k)
                base_before, base = base_of(b), base_of(b + 1)
                for t in range(0, tiles, QUAD):
                    ins = dve.tensor_tensor(
                        onehot[:, par, t:t + QUAD, :], k.iota[:].unsqueeze(1).broadcast_to([P, QUAD, P]),
                        k.near[:, cols(b * BT + t, QUAD)].unsqueeze(2).broadcast_to([P, QUAD, P]), ALU.is_equal)
                st.done(ins)
                scores(b, i, par, st, lambda: add_window(b, base_before, st))
                dve.wait_ge(p_done, b + 3)
                for t in range(0, tiles, QUAD):
                    quad = ring[:, par * BT + t:par * BT + t + QUAD, :]
                    rows = quad[:, :, 0:D].rearrange("p t (h d) -> p t h d", h=HEADS)
                    dve.tensor_tensor(rows, rows, quad[:, :, D:ROW1].unsqueeze(3).broadcast_to(
                        [P, QUAD, HEADS, HD]), ALU.mult).then_inc(weighted, 1)
                fade_open(b, base, st)
                if tiles == LAST_TILES:
                    add_window(b + 1, base, st)

            def general(i, par, tiles):
                b = 2 * i + par
                st = Steps(dve, s, (SCORES + FADES) * b, k)
                scores(b, i, par, st)
                _, bases = nc.values_load_multi_w_load_instructions(
                    k.base[0:1, cols(b * BT + BT, tiles)], engines=[dve.engine], min_val=0, max_val=COLS - P)
                dve.wait_ge(added[BT - 1], b + 1)
                fade_open(b, bases[0], st)

                def one_hot(t):
                    dve.wait_ge(used[(t - 4) % BT], b + 3 if t >= 4 else b + 2)
                    dve.tensor_scalar(onehot[:, 0, t % 4, :], k.iota[:], off[par][:, t:t + 1], None, ALU.is_equal
                                      ).then_inc(hot[t], 1)
                    rows = ring[:, par * BT + t, 0:D].rearrange("p (h d) -> p h d", h=HEADS)
                    dve.tensor_tensor(rows, rows, prob[:, t:BT * HEADS:BT].unsqueeze(2).broadcast_to(
                        [P, HEADS, HD]), ALU.mult).then_inc(hot[t], 1)

                dve.wait_ge(p_done, b + 3)
                dve.wait_ge(staged, b + 1)
                one_hot(0)
                one_hot(1)
                for t in range(tiles):
                    if t + 2 < tiles:
                        one_hot(t + 2)
                    dve.wait_ge(used[t], b + 3)
                    dve.wait_ge(added[(t - 1) % BT], b + 2 if t else b + 1)
                    sums = k.acc[:, :, cols(bases[t], P)]
                    sums_s = k.acc_s[:, cols(bases[t], P)]
                    dve.tensor_tensor(sums_s, sums_s, win[t % 4][0:HEADS, 2, :], ALU.add)
                    dve.tensor_tensor(sums, sums, win[t % 4][:, 0:H, :], ALU.add).then_inc(added[t], 1)
                if tiles == LAST_TILES:
                    dve.wait_ge(added[LAST_TILES - 1], BATCHES + 1)
            either(dve, narrow, general)


def ffn1(nc, k, g, out):
    X = EXPERTS
    CH = H
    with ExitStack() as ctx:
        a = allocator(nc, ctx)
        wa, wb, wo = (a.sb(n, [P, X, H, D]) for n in ("wa", "wb", "wo"))
        wr = a.sb("wr1", [P, H, X])
        br = a.sb("br1", [P, X])
        bo = a.sb("bo", [X, D])
        bn_par = a.sb("bn_rows", [X * CH, 10, P])
        bn_t = a.sb("bn_tmp", [X * CH, 4, P])
        bn = a.sb("bn", [P, 4, X * CH])
        y = a.sb("y", [P, NODE_TILES, D])
        gate = a.sb("gate", [P, NODE_TILES, X])
        xn = a.sb("exn", [P, D])
        agg = a.sb("agg", [P, D])
        rden, lg, ex = a.sb("rden", [P, HEADS]), a.sb("lg", [P, X]), a.sb("ex", [P, X])
        nmax, esum = a.sb("nmax", [P, 1]), a.sb("esum", [P, 1])
        gate_n, gate_t = a.sb("gate_n", [P, X]), a.sb("gate_t", [X, P])
        sums, sums_s = a.sb("esums", [P, H, P]), a.sb("esums_s", [HEADS, P])
        xt = a.sb("ext", [P, H, P])
        norm_ = Norm(a, k, "e")
        h1 = [a.sb(f"h1_{i}", [P, CH, GCOLS]) for i in range(2)]
        h2 = [a.sb(f"h2_{i}", [P, CH, GCOLS]) for i in range(2)]
        p1 = [a.bank(f"p1_{i}", GCOLS) for i in range(CH)]
        p2 = [a.bank(f"p2_{i}", GCOLS) for i in range(CH)]
        py = [a.bank(f"py_{i}", D) for i in range(2)]
        f_ps = a.bank("f_ps", 4, P)
        g_ps = a.bank("g_ps", 4, P)
        w_load, p_load, y_load = a.sem("w_load"), a.sem("p_load"), a.sem("y_load")
        s, bn_turned, bn_ready = a.sem("esteps"), a.sem("bn_turned"), a.sem("bn_ready")
        bn_steps = a.sem("bn_steps")
        m1, k1, m2, k2 = a.sem("m1s"), a.sem("k1s"), a.sem("m2s"), a.sem("k2s")
        ym, yt = a.sem("ym"), a.sem("yt")
        pe_fin, act_fin, to_pe, to_act = a.sem("pe_fin"), a.sem("act_fin"), a.sem("fin_pe"), a.sem("fin_act")
        o_sem = a.sem("out_stored")
        block = ctx.enter_context(nc.Block())
        rows16 = "e (c p) -> (e c) p"
        names = ["v1", "g1", "b1", "m1", "be1", "v2", "g2", "b2", "m2", "be2"]
        whole = (NODE_TILES - 1) * P
        FIN0 = 4 + Norm.STEPS_ALONE
        FPER = FIN0 + 7
        PE_FIN, TO_PE, ACT_FIN = 5, 3, 5

        order = []
        for e in range(X + 2):
            order += [(1, e)] * (e < X) + [(2, e - 1)] * (1 <= e <= X) + [(3, e - 2)] * (e >= 2)
        STAGES = 5

        def weave(gi, mine, ahead, piece, fin):
            todo = [(stage, t, r) for t, r in enumerate(ahead) for stage in range(STAGES)]
            for layer, e in order if mine else ():
                piece(gi, layer, e, mine)
                if todo:
                    stage, t, r = todo.pop(0)
                    fin(gi + 1, stage, t, r)
            for stage, t, r in todo:
                fin(gi + 1, stage, t, r)

        def all_groups(eng, piece, fin):
            weave(-1, [], [P] * GROUP, piece, fin)
            with eng.Fori(0, GROUPS - 1) as i:
                weave(i, [P] * GROUP, [P] * GROUP, piece, fin)
            weave(GROUPS - 1, [P] * GROUP, [LAST_ROWS], piece, fin)
            weave(GROUPS, [LAST_ROWS], [], piece, fin)

        def y_count(gi, e, t, mine):
            return GROUP * X * gi + len(mine) * e + t

        @block.sync
        def _(sp):
            sp.dma_start(y[:, 0:NODE_TILES - 1, :], k.x2_d[0:whole, :].rearrange("(t p) d -> p t d", p=P)
                         ).then_inc(y_load, 16)
            sp.dma_start(y[:LAST_ROWS, NODE_TILES - 1, :], k.x2_d[whole:N, :]).then_inc(y_load, 16)
            for i, n in enumerate(names):
                sp.dma_start(bn_par[:, i, :], g[f"L1_ffn_{n}"].rearrange(rows16, p=P)).then_inc(p_load, 16)
            sp.dma_start(wr[:], g["L1_ffn_Wr"].rearrange("(h p) x -> p h x", p=P)).then_inc(p_load, 16)
            sp.dma_start(br[:], g["L1_ffn_br"].rearrange("(a x) -> a x", a=1).broadcast_to([P, X])
                         ).then_inc(p_load, 16)
            sp.dma_start(bo[:], g["L1_ffn_bo"]).then_inc(p_load, 16)
            for w, n in ((wa, "W1"), (wb, "W2"), (wo, "Wo")):
                for e in range(X):
                    sp.dma_start(w[:, e, :, :], g[f"L1_ffn_{n}"][e].rearrange("(h p) d -> p h d", p=P)
                                 ).then_inc(w_load, 16)
            with sp.Fori(0, GROUPS) as gi:
                sp.wait_ge(yt, GROUP * X * gi + GROUP * X + 2)
                sp.dma_start(out[cols(gi * GCOLS, GCOLS), :].rearrange("(t p) d -> p t d", p=P),
                             y[:, cols(gi * GROUP, GROUP), :]).then_inc(o_sem, 16)
            sp.wait_ge(yt, GROUP * X * GROUPS + X + 2)
            sp.dma_start(out[whole:N, :], y[:LAST_ROWS, NODE_TILES - 1, :]).then_inc(o_sem, 16)
            sp.wait_ge(o_sem, 16 * (GROUPS + 1))

        @block.tensor
        def _(pe):
            pe.sem_inc(k1, 2)
            pe.sem_inc(k2, 2)
            pe.sem_inc(yt, 2)
            pe.wait_ge(bn_ready, 1)
            for i in range(4):
                ins = pe.transpose(g_ps[:, i, 0:X * CH], bn_t[:, i, :], k.ident[0:X * CH, 0:X * CH])
            ins.then_inc(bn_turned, 1)
            pe.wait_ge(bn_ready, 2)
            pe.wait_ge(p_load, 16 * 13)

            def fin(gi, stage, t, r):
                n = GROUP * gi + t
                if stage == 0:
                    pe.wait_ge(act_fin, ACT_FIN * n + 2)
                    if not (isinstance(n, int) and n == 0):
                        pe.wait_ge(s, FPER * n)
                    for h in range(H):
                        pe.transpose(f_ps[:r, h, :], sums[:, h, :r], k.ident[:])
                    pe.transpose(g_ps[:r, 2, 0:HEADS], sums_s[:, :r],
                                 k.ident[0:HEADS, 0:HEADS]).then_inc(pe_fin, 1)
                if stage == 1:
                    pe.wait_ge(to_pe, TO_PE * n + 1)
                    for h in range(H):
                        ins = pe.transpose(f_ps[:, 2 + h, :r], xn[:r, h * P:(h + 1) * P], k.ident[:r, :r])
                    ins.then_inc(pe_fin, 1)
                if stage == 2:
                    pe.wait_ge(act_fin, ACT_FIN * n + 3)
                    for h in range(H):
                        ins = pe.matmul(g_ps[:r, 2, 0:X], xt[:, h, :r], wr[:, h, :],
                                        start=(h == 0), stop=(h == H - 1))
                    ins.then_inc(pe_fin, 1)
                if stage == 3:
                    pe.wait_ge(to_pe, TO_PE * n + 2)
                    pe.transpose(g_ps[0:X, 2, :r], gate_n[:r, :], k.ident[:r, :r]).then_inc(pe_fin, 1)
                if stage == 4:
                    pe.wait_ge(to_pe, TO_PE * n + 3)
                    pe.matmul(g_ps[:r, 0:2, :].rearrange("p a b -> p (a b)"), gate_t[:, :r], bo[:],
                              start=True, stop=True).then_inc(pe_fin, 1)

            def piece(gi, layer, e, mine):
                m = sum(mine)
                if layer == 1:
                    if e == 0:
                        pe.wait_ge(act_fin, ACT_FIN * (GROUP * gi + len(mine)))
                    for c in range(CH):
                        pe.wait_ge(k1, CH * X * gi + CH * e + c + 1)
                        for h in range(H):
                            ins = pe.matmul(p1[c][:, :m], wa[:, e, h, c * P:(c + 1) * P],
                                            k.acc[:, h, cols(gi * GCOLS, m)], start=(h == 0), stop=(h == H - 1))
                        ins.then_inc(m1, 1)
                elif layer == 2:
                    pe.wait_ge(k1, CH * X * gi + CH * e + CH + 2)
                    for c in range(CH):
                        pe.wait_ge(k2, CH * X * gi + CH * e + c + 1)
                        for h in range(CH):
                            ins = pe.matmul(p2[c][:, :m], wb[:, e, h, c * P:(c + 1) * P],
                                            h1[e % 2][:, h, :m], start=(h == 0), stop=(h == CH - 1))
                        ins.then_inc(m2, 1)
                else:
                    pe.wait_ge(k2, CH * X * gi + CH * e + CH + 2)
                    for t, r in enumerate(mine):
                        q = y_count(gi, e, t, mine)
                        pe.wait_ge(yt, q + 1)
                        b = (t if len(mine) > 1 else e) % 2
                        for h in range(CH):
                            ins = pe.matmul(py[b][:r, 0:D], h2[e % 2][:, h, t * P:t * P + r], wo[:, e, h, :],
                                            start=(h == 0), stop=(h == CH - 1))
                        ins.then_inc(ym, 1)

            weights = [0]

            def piece_after_load(gi, layer, e, mine):
                if not weights[0]:
                    weights[0] = 1
                    pe.wait_ge(w_load, 16 * 3 * X)
                piece(gi, layer, e, mine)

            all_groups(pe, piece_after_load, fin)

        @block.scalar
        def _(act):
            act.wait_ge(bn_ready, 2)

            def fin(gi, stage, t, r):
                n = GROUP * gi + t
                here = cols(gi * GCOLS + t * P, r)
                if stage == 0:
                    act.copy(sums[:, :, :r], k.acc[:, :, here]).then_inc(act_fin, 1)
                    act.copy(sums_s[:, :r], k.acc_s[:, here]).then_inc(act_fin, 1)
                if stage == 1:
                    act.wait_ge(pe_fin, PE_FIN * n + 2)
                    act.copy(xt[:, :, :r], f_ps[:, 2:4, :r]).then_inc(act_fin, 1)
                    act.copy(k.acc[:, :, here], f_ps[:, 2:4, :r]).then_inc(act_fin, 1)
                if stage == 2:
                    act.wait_ge(to_act, n + 1)
                    act.activation(ex[:r, :], lg[:r, :], ACT.Exp, bias=nmax[:r, :], accum_out=esum[:r, :]
                                   ).then_inc(act_fin, 1)

            def piece(gi, layer, e, mine):
                m = sum(mine)
                if layer == 3:
                    return
                made, kept, src, dst, j = ((m1, k1, p1, h1, 0), (m2, k2, p2, h2, 2))[layer - 1]
                for c in range(CH):
                    act.wait_ge(made, CH * X * gi + CH * e + c + 1)
                    q = CH * e + c
                    act.activation(dst[e % 2][:, c, :m], src[c][:, :m], ACT.Relu, scale=bn[:, j, q:q + 1],
                                   bias=bn[:, j + 1, q:q + 1]).then_inc(kept, 1)
            all_groups(act, piece, fin)

        @block.vector
        def _(dve):
            st = Steps(dve, bn_steps, 0, k)
            dve.wait_ge(p_load, 16 * 13)
            for j in range(2):
                v = bn_par[:, 5 * j, :]
                st.then(dve.tensor_scalar(v, v, BN_EPS, None, ALU.add))
                inverse_root(dve, st, v, bn_t[:, 2 * j, :], bn_t[:, 2 * j + 1, :])
            for j in range(2):
                _, gam, b, mean, beta = (bn_par[:, 5 * j + i, :] for i in range(5))
                scale, shift = bn_t[:, 2 * j, :], bn_t[:, 2 * j + 1, :]
                st.done(dve.tensor_tensor(shift, b, mean, ALU.subtract))
                st.then(dve.tensor_tensor(scale, scale, gam, ALU.mult))
                st.then(dve.tensor_tensor(shift, shift, scale, ALU.mult))
                st.then(dve.tensor_tensor(shift, shift, beta, ALU.add))
            dve.sem_inc(bn_ready, 1)
            dve.wait_ge(bn_turned, 1)
            st.then(dve.tensor_copy(bn[:], g_ps[:, :, 0:X * CH]))
            dve.sem_inc(bn_ready, 1)
            dve.wait_ge(y_load, 32)

            def fin(gi, stage, t, r):
                n = GROUP * gi + t
                st = Steps(dve, s, FPER * n + (0, FIN0, FIN0, FIN0 + 5, FIN0 + 6)[stage], k)
                row = y[:r, cols(n, 1), :].rearrange("p a d -> p (a d)")
                if stage == 0:
                    dve.wait_ge(pe_fin, PE_FIN * n + 1)
                    st.then(dve.tensor_scalar(rden[:r, :], g_ps[:r, 2, 0:HEADS], 1e-16, None, ALU.add))
                    st.then(dve.reciprocal(rden[:r, :], rden[:r, :]))
                    st.then(dve.tensor_tensor(
                        agg[:r, :].rearrange("p (h d) -> p h d", h=HEADS),
                        f_ps[:r, 0:H, :].rearrange("p a (b d) -> p (a b) d", d=HD),
                        rden[:r, :].unsqueeze(2).broadcast_to([r, HEADS, HD]), ALU.mult))
                    st.then(dve.tensor_tensor(row, row, agg[:r, :], ALU.add))
                    norm_.apply_alone(dve, st, row, xn[:r, :], r)
                    assert st.n == FIN0
                    dve.sem_inc(to_pe, 1)
                if stage == 2:
                    dve.wait_ge(pe_fin, PE_FIN * n + 3)
                    st.then(dve.tensor_tensor(lg[:r, :], g_ps[:r, 2, 0:X], br[:r, :], ALU.add))
                    st.then(dve.tensor_reduce(nmax[:r, :], lg[:r, :], AX, ALU.max, negate=True))
                    dve.sem_inc(to_act, 1)
                    dve.wait_ge(act_fin, ACT_FIN * n + 5)
                    st.then(dve.reciprocal(esum[:r, :], esum[:r, :]))
                    st.done(dve.tensor_scalar(gate[:r, cols(n, 1), :].rearrange("p a x -> p (a x)"), ex[:r, :],
                                              esum[:r, 0:1], None, ALU.mult))
                    st.then(dve.tensor_scalar(gate_n[:r, :], ex[:r, :], esum[:r, 0:1], None, ALU.mult))
                    dve.sem_inc(to_pe, 1)
                if stage == 3:
                    dve.wait_ge(pe_fin, PE_FIN * n + 4)
                    st.then(dve.tensor_copy(gate_t[:, :r], g_ps[0:X, 2, :r]))
                    dve.sem_inc(to_pe, 1)
                if stage == 4:
                    dve.wait_ge(pe_fin, PE_FIN * n + 5)
                    st.then(dve.tensor_tensor(row, row, g_ps[:r, 0:2, :].rearrange("p a b -> p (a b)"), ALU.add))

            def piece(gi, layer, e, mine):
                if layer != 3:
                    return
                for t, r in enumerate(mine):
                    n = GROUP * gi + t
                    q = y_count(gi, e, t, mine)
                    b = (t if len(mine) > 1 else e) % 2
                    dve.wait_ge(ym, q + 1)
                    if e == 0:
                        if t == 0:
                            dve.wait_ge(s, FPER * (GROUP * gi + len(mine)))
                    else:
                        dve.wait_ge(yt, q - len(mine) + 3)
                    row = y[:r, cols(n, 1), :].rearrange("p a d -> p (a d)")
                    dve.scalar_tensor_tensor(row, py[b][:r, 0:D], gate[:r, cols(n, 1), e:e + 1].rearrange(
                        "p a x -> p (a x)"), row, ALU.mult, ALU.add).then_inc(yt, 1)
            all_groups(dve, piece, fin)


def build(nc, g, out):
    with ExitStack() as ctx:
        a = allocator(nc, ctx)
        k = Named()

        def dram(name, shape, dt=F32):
            return nc.dram_tensor(name, shape, dt, kind="Internal").ap()
        k.table0_d = dram("table0", (RELS * NP, D))
        k.table1_d = dram("table1", (N, ROW1))
        k.x1_d, k.x2_d = dram("x1", (NP, D)), dram("x2", (NP, D))
        k.starts_d = dram("starts_d", (HEADS, TPAD, P + 1))
        k.ends_d, k.both_d = dram("ends_d", (TPAD, 2)), dram("both_d", (TPAD,))
        k.base_d, k.base_f_d = dram("base_d", (TPAD,), I32), dram("base_f_d", (TPAD,))

        k.acc = a.sb("acc", [P, H, COLS])
        k.acc_s = a.sb("acc_s", [HEADS, COLS])
        k.got0, k.got1 = a.sems("got0_", 2 * BT), a.sems("got1_", 2 * BT)
        k.passed = a.sem("passed")
        k.ident, k.iota = a.sb("ident", [P, P]), a.sb("iota", [P, P])
        k.head_of, k.head_of_t = a.sb("head_of", [P, HEADS]), a.sb("head_of_t", [HEADS, P])
        k.tile_of, k.head_rows = a.sb("tile_of", [P, BT]), a.sb("head_rows", [HEADS, D])
        k.ones = a.sb("ones", [1, P])
        k.eps = a.sb("eps", [P, 1])
        k.node_sums = a.sb("node_sums", [P, H, NODE_TILES])
        constants(nc, k)
        with ExitStack() as graph:
            b = allocator(nc, graph)
            k.meta = b.sb("meta", [P, 4, TPAD])
            k.base = b.sb("base", [1, BT + TPAD], I32)
            k.near = b.sb("near", [P, TPAD])
            k.narrow = b.sb("narrow", [1, 1], I32)
            k.ends8, k.both8 = b.sb("ends8", [HEADS, 2 * TPAD]), b.sb("both8", [HEADS, TPAD])
            edge_tables(nc, k, g)
            relation_table(nc, k, g)
            gnn0_edges(nc, k)
            gnn0_nodes(nc, k, g)
            with ExitStack() as experts:
                c = allocator(nc, experts)
                k.w1 = c.sb("w1", [P, 2, H, F0])
                k.w2 = c.sb("w2", [P, 2, F0 // P, D])
                k.b1, k.b2 = c.sb("b1", [P, 2, F0 // P]), c.sb("b2", [1, D])
                route(nc, k, g)
                ffn0(nc, k, g)
            gnn1_edges(nc, k)
        ffn1(nc, k, g, out)


NAMES = ["x", "src", "dst", "edge_type_8", "edge_weight", "L0_gnn_weight", "L0_ffn_Wr", "L0_ffn_br",
         "L0_ffn_W1", "L0_ffn_b1", "L0_ffn_W2", "L0_ffn_b2", "L0_ffn_gamma", "L0_ffn_beta", "L1_gnn_W",
         "L1_gnn_a_src", "L1_gnn_a_dst", "L1_ffn_Wr", "L1_ffn_br", "L1_ffn_W1", "L1_ffn_b1", "L1_ffn_g1",
         "L1_ffn_be1", "L1_ffn_m1", "L1_ffn_v1", "L1_ffn_W2", "L1_ffn_b2", "L1_ffn_g2", "L1_ffn_be2",
         "L1_ffn_m2", "L1_ffn_v2", "L1_ffn_Wo", "L1_ffn_bo"]


def kernel(**inputs):
    import concourse.bacc as bacc
    from concourse.bass_utils import run_bass_kernel_spmd

    nc = bacc.Bacc("TRN2", target_bir_lowering=False, num_devices=1)
    arrays, g = {}, {}
    for name in NAMES:
        arr = np.ascontiguousarray(inputs[name])
        arrays[f"in_{name}"] = arr
        g[name] = nc.dram_tensor(f"in_{name}", arr.shape, mybir.dt.from_np(arr.dtype), kind="ExternalInput").ap()
    out = nc.dram_tensor("out", (N, D), F32, kind="ExternalOutput").ap()
    build(nc, g, out)
    r = run_bass_kernel_spmd(nc, [arrays], core_ids=[0])
    return r.results[0]["out"]
```

```python
from contextlib import ExitStack

import numpy as np

import concourse.bass as bass
from concourse import mybir

ALU = mybir.AluOpType
ACT = mybir.ActivationFunctionType
AX = mybir.AxisListType.X
F32 = mybir.dt.float32
I32 = mybir.dt.int32

P = 128
N = 6250
D = 256
H = D // P
E = 206250
RELS = 8
HEADS = 8
HD = D // HEADS
EXPERTS = 8
F0 = 512

NODE_TILES = -(-N // P)
NP = NODE_TILES * P
LAST_ROWS = N - (NODE_TILES - 1) * P
GROUP = 4
GCOLS = GROUP * P
GROUPS = NODE_TILES // GROUP
assert NODE_TILES == GROUPS * GROUP + 1

TILES = -(-E // P)
BT = 16
BATCHES = -(-TILES // BT)
LAST_TILES = TILES - (BATCHES - 1) * BT
assert BATCHES % 2 == 1
BLOCKS = -(-TILES // P)
TPAD = BLOCKS * P
PAD_NODE = N
COLS = -(-(N + P) // P) * P

BANK = 512
ROW1 = D + HEADS
BIG = 1.0e38
LN_EPS = 1e-5
BN_EPS = 1e-3
CAPACITY = float(-(-(N * 5) // (4 * EXPERTS)))


class Named:
    pass


def allocator(nc, ctx):
    a = Named()
    a.sb = lambda name, shape, dt=F32: ctx.enter_context(nc.sbuf_tensor(name, shape, dt))
    a.ps = lambda name, shape: ctx.enter_context(nc.psum_tensor(name, shape, F32))

    def bank(name, *shape):
        n = int(np.prod(shape))
        v = a.ps(name, [P, BANK])[:, 0:n]
        return v if len(shape) == 1 else v.rearrange("p (a b) -> p a b", b=shape[-1])
    a.bank = bank
    held = []

    def sem(name):
        held.append(nc.alloc_semaphore(name))
        return held[-1]

    def release():
        if held:
            nc.clear_and_free_semaphores(held)
            nc.all_engine_barrier()
    ctx.callback(release)
    a.sem = sem
    a.sems = lambda name, n: [a.sem(f"{name}{i}") for i in range(n)]
    return a


class Steps:

    def __init__(self, eng, sem, base=0, k=None):
        self.eng, self.sem, self.base, self.n, self.k = eng, sem, base, 0, k

    def done(self, ins):
        ins.then_inc(self.sem, 1)
        self.n += 1

    def wait(self):
        self.eng.wait_ge(self.sem, self.base + self.n)

    def then(self, ins):
        self.done(ins)
        self.wait()


def node_pairs(eng, emit):
    with eng.Fori(0, NODE_TILES // 2) as i:
        emit(i, 0, P)
        emit(i, 1, P)
    emit(NODE_TILES // 2, 0, LAST_ROWS)


def batch_pairs(eng, emit):
    with eng.Fori(0, BATCHES // 2) as i:
        emit(i, 0, BT)
        emit(i, 1, BT)
    emit(BATCHES // 2, 0, LAST_TILES)


def cols(start, n):
    return bass.ds(start, n)


def inverse_root(dve, st, x, guess, t):
    past_waits(dve, st.k)
    st.then(dve.tensor_scalar(t.bitcast(I32), x.bitcast(I32), 1, None, ALU.arith_shift_right))
    st.then(dve.tensor_scalar(guess.bitcast(I32), t.bitcast(I32), -1.0, float(0x5f3759df), ALU.mult, ALU.add))
    for _ in range(3):
        st.then(dve.tensor_tensor(t, guess, guess, ALU.mult))
        st.then(dve.tensor_tensor(t, t, x, ALU.mult))
        st.then(dve.tensor_scalar(t, t, -0.5, 1.5, ALU.mult, ALU.add))
        st.then(dve.tensor_tensor(guess, guess, t, ALU.mult))


INVERSE_ROOT_STEPS = 14


class Norm:
    STEPS = 3

    def __init__(self, a, k, name):
        self.stats, self.mv = a.sb(name + "stats", [P, 6]), a.sb(name + "mv", [P, 2])
        self.rstd, self.tmp = a.sb(name + "rstd", [P, 1]), a.sb(name + "tmp", [P, 1])
        self.asked, self.rooted = a.sem(name + "asked"), a.sem(name + "rooted")
        self.k = k

    def apply(self, dve, st, m, x, out, r, meanwhile=lambda: None):
        past_waits(dve, self.k)
        st.then(dve.bn_stats(self.stats[:r, :], x))
        past_waits(dve, self.k)
        dve.bn_aggr(self.mv[:r, :], self.stats[:r, :]).then_inc(self.asked, 1)
        meanwhile()
        dve.wait_ge(self.rooted, m + 1)
        st.then(dve.reciprocal(self.rstd[:r, :], self.rstd[:r, :]))
        st.then(dve.tensor_scalar(out, x, self.mv[:r, 0:1], self.rstd[:r, 0:1], ALU.subtract, ALU.mult))

    def root(self, act, m, r):
        act.wait_ge(self.asked, m + 1)
        act.activation(self.rstd[:r, :], self.mv[:r, 1:2], ACT.Sqrt, bias=self.k.eps[:r, :]
                       ).then_inc(self.rooted, 1)


def past_waits(eng, k):
    eng.sem_inc(k.passed, 1)


def load_tables(act, k, func):
    act.activation(k.unused[:], k.eps[:], func)


def constants(nc, k):
    with ExitStack() as ctx:
        a = allocator(nc, ctx)
        diff = a.sb("diff", [P, P], I32)
        column = a.sb("column", [P, P], I32)
        made, s = a.sem("iota_made"), a.sem("const_steps")
        t_ps = a.bank("t_ps", P)
        t_done = a.sem("e8t_turned")
        block = ctx.enter_context(nc.Block())

        @block.gpsimd
        def _(pool):
            pool.iota(diff[:], [[1, P]], base=0, channel_multiplier=-1).then_inc(made, 1)
            pool.iota(column[:], [[1, P]], base=0, channel_multiplier=0).then_inc(made, 1)

        @block.tensor
        def _(pe):
            pe.wait_ge(s, 4)
            pe.transpose(t_ps[0:HEADS, :], k.head_of[:], k.ident[:]).then_inc(t_done, 1)

        @block.vector
        def _(dve):
            st = Steps(dve, s, 0, k)
            dve.wait_ge(made, 2)
            st.then(dve.tensor_scalar(k.ident[:], diff[:], 0.0, None, ALU.is_equal))
            st.then(dve.tensor_copy(k.iota[:], column[:]))
            st.then(dve.tensor_reduce(k.head_of[:], k.ident[:].rearrange("p (h t) -> p h t", h=HEADS),
                                      AX, ALU.add))
            st.then(dve.tensor_reduce(k.tile_of[:], k.ident[:].rearrange("p (h t) -> p t h", h=HEADS),
                                      AX, ALU.add))
            st.done(dve.tensor_copy(k.head_rows[:].rearrange("h (g c) -> h g c", c=HD),
                                    k.ident[0:HEADS, 0:HEADS].unsqueeze(2).broadcast_to([HEADS, HEADS, HD])))
            st.done(dve.memset(k.ones[:], 1.0))
            st.done(dve.memset(k.eps[:], LN_EPS))
            dve.wait_ge(t_done, 1)
            st.done(dve.tensor_copy(k.head_of_t[:], t_ps[0:HEADS, :]))
            st.wait()


def edge_tables(nc, k, g):
    whole, rest = (TILES // P) * P * P, E % P
    rows = TILES - 1 - (TILES // P) * P
    with ExitStack() as ctx:
        a = allocator(nc, ctx)
        dst_i = a.sb("dst_i", [P, BLOCKS, P], I32)
        src_i = a.sb("src_i", [P, BLOCKS, P], I32)
        rel_i = a.sb("rel_i", [P, BLOCKS, P], I32)
        prev_i = a.sb("prev_i", [P, BLOCKS], I32)
        weight = a.sb("weight", [P, BLOCKS, P])
        row0 = a.sb("row0", [P, BLOCKS, P])
        src_f = a.sb("src_f", [P, BLOCKS, P])
        off_f = a.sb("off_f", [P, BLOCKS, P])
        dst_f = a.sb("dst_f", [P, BLOCKS, P])
        prev_f = a.sb("prev_f", [P, BLOCKS])
        starts = k.starts
        ends = a.sb("ends", [P, BLOCKS, 2])
        both = a.sb("both", [P, BLOCKS])
        base_c, base_f = a.sb("base_c", [P, BLOCKS], I32), a.sb("base_f", [P, BLOCKS])
        base_row = a.sb("base_row", [P, TPAD])
        far = a.sb("far", [P, 1])
        turned = a.ps("turned", [P, 2, 4, P])
        filled, loaded = a.sem("filled"), a.sem("edges_loaded")
        s, ready = a.sem("edge_steps"), a.sem("edge_arrays")
        turn, taken = a.sem("turned_q"), a.sem("taken_q")
        stored, back = a.sem("edge_stored"), a.sem("edge_back")
        block = ctx.enter_context(nc.Block())

        def flat(ap):
            return ap.rearrange("(k q e) -> q k e", q=P, e=P)

        loads = []
        for name, t in (("dst", dst_i), ("src", src_i), ("edge_type_8", rel_i), ("edge_weight", weight)):
            arr = g[name]
            loads += [(t[:, 0:BLOCKS - 1, :], flat(arr[0:whole])),
                      (t[0:rows, BLOCKS - 1, :], arr[whole:whole + rows * P].rearrange("(q e) -> q e", e=P)),
                      (t[rows:rows + 1, BLOCKS - 1, 0:rest],
                       arr[E - rest:E].rearrange("(q e) -> q e", e=rest))]
        before = g["dst"][0:(TILES - 1) * P].rearrange("(t e) -> t e", e=P)[:, P - 1:P]
        loads += [(prev_i[1:P, 0:1], before[0:P - 1, :])]
        for b in range(1, BLOCKS):
            n = min(P, TILES - b * P)
            loads += [(prev_i[0:n, b:b + 1], before[b * P - 1:b * P - 1 + n, :])]

        @block.gpsimd
        def _(pool):
            pool.memset(k.base[:, 0:BT], 0).then_inc(filled, 1)
            for t, v in ((dst_i, PAD_NODE), (src_i, 0), (rel_i, 0)):
                pool.memset(t[:, BLOCKS - 1, :], v).then_inc(filled, 1)
            pool.memset(weight[:, BLOCKS - 1, :], 0.0).then_inc(filled, 1)
            pool.memset(prev_i[:], PAD_NODE).then_inc(filled, 1)
            pool.memset(starts[:], 0.0).then_inc(filled, 1)
            pool.wait_ge(filled, 7)
            pool.memset(prev_i[0:1, 0:1], -1).then_inc(filled, 1)
            pool.wait_ge(filled, 8)

        @block.sync
        def _(sp):
            sp.wait_ge(filled, 8)
            with nc.allow_non_contiguous_dma(reason="one destination per tile"):
                for dst, src in loads:
                    sp.dma_start(dst, src).then_inc(loaded, 16)
            sp.wait_ge(ready, 1)
            with nc.allow_non_contiguous_dma(reason="one base per tile"):
                sp.dma_start(k.ends_d.rearrange("(k q) e -> q k e", q=P), ends[:]).then_inc(stored, 16)
                sp.dma_start(k.both_d.rearrange("(k q) -> q k", q=P), both[:]).then_inc(stored, 16)
                sp.dma_start(k.base_d.rearrange("(k q) -> q k", q=P), base_c[:]).then_inc(stored, 16)
                sp.dma_start(k.base_f_d.rearrange("(k q) -> q k", q=P), base_f[:]).then_inc(stored, 16)
            sp.wait_ge(stored, 64)
            flat_ends = k.ends_d.rearrange("(a t) e -> a (t e)", a=1)
            sp.dma_start(k.ends8[:], flat_ends.broadcast_to([HEADS, 2 * TPAD])).then_inc(back, 16)
            sp.dma_start(k.both8[:], k.both_d.rearrange("(a t) -> a t", a=1).broadcast_to([HEADS, TPAD])
                         ).then_inc(back, 16)
            sp.dma_start(k.base[:, BT:BT + TPAD], k.base_d.rearrange("(a t) -> a t", a=1)).then_inc(back, 16)
            sp.dma_start(base_row[:], k.base_f_d.rearrange("(a t) -> a t", a=1).broadcast_to([P, TPAD])
                         ).then_inc(back, 16)
            sp.wait_ge(back, 64)

        @block.scalar
        def _(act):
            act.wait_ge(ready, 1)
            for h in range(HEADS):
                act.dma_start(k.starts_d[h].rearrange("(k q) e -> q k e", q=P), starts[:]
                              ).then_inc(k.starts_stored, 16)

        @block.vector
        def _(dve):
            st = Steps(dve, s, 0, k)
            st.done(dve.memset(k.acc[:], 0.0))
            dve.wait_ge(loaded, 16 * len(loads))
            st.done(dve.tensor_copy(dst_f[:], dst_i[:]))
            st.done(dve.tensor_copy(prev_f[:], prev_i[:]))
            st.done(dve.tensor_copy(base_c[:], dst_i[:, :, 0]))
            st.done(dve.tensor_copy(base_f[:], dst_i[:, :, 0]))
            st.done(dve.scalar_tensor_tensor(row0[:], rel_i[:], float(NP), src_i[:], ALU.mult, ALU.add))
            st.then(dve.tensor_copy(src_f[:], src_i[:]))
            st.done(dve.tensor_tensor(off_f[:], dst_f[:], dst_f[:, :, 0:1].broadcast_to([P, BLOCKS, P]),
                                      ALU.subtract))
            st.done(dve.tensor_tensor(starts[:, :, 1:P], dst_f[:, :, 1:P], dst_f[:, :, 0:P - 1],
                                      ALU.not_equal))
            st.done(dve.tensor_tensor(starts[:, :, 0], dst_f[:, :, 0], prev_f[:], ALU.not_equal))
            st.done(dve.tensor_tensor(ends[:, :, 0], dst_f[:, :, 0], prev_f[:], ALU.not_equal))
            st.then(dve.tensor_tensor(ends[:, :, 1], dst_f[:, :, P - 1], dst_f[:, :, 0], ALU.not_equal))
            st.done(dve.tensor_scalar(starts[:], starts[:], -BIG, None, ALU.mult))
            st.then(dve.tensor_scalar(ends[:], ends[:], -BIG, None, ALU.mult))
            st.then(dve.tensor_tensor(both[:], ends[:, :, 0], ends[:, :, 1], ALU.add))
            dve.sem_inc(ready, 1)
            n = 0
            for kind in range(4):
                for b in range(0, BLOCKS, 4):
                    m = min(4, BLOCKS - b)
                    dve.wait_ge(turn, n + 1)
                    st.then(dve.tensor_copy(k.meta[:, kind, b * P:(b + m) * P],
                                            turned[:, n % 2, 0:m, :].rearrange("p a b -> p (a b)")))
                    dve.sem_inc(taken, 1)
                    n += 1
            dve.wait_ge(back, 64)
            st.then(dve.tensor_tensor(k.near[:], k.meta[:, OFF_KIND, :], base_row[:], ALU.add))
            near = k.near[:].rearrange("p (b t) -> p b t", t=BT)
            first = base_row[:].rearrange("p (b t) -> p b t", t=BT)[:, :, 0:1]
            st.then(dve.tensor_tensor(near, near, first.broadcast_to([P, TPAD // BT, BT]), ALU.subtract))
            st.then(dve.tensor_reduce(far[:], k.near[:], AX, ALU.max))
            dve.sem_inc(taken, 1)
            dve.wait_ge(turn, n + 1)
            st.then(dve.tensor_reduce(far[0:1, :], turned[0:1, 0, 0, :], AX, ALU.max))
            st.then(dve.tensor_scalar(k.narrow[:], far[0:1, :], float(P), None, ALU.is_lt))

        @block.tensor
        def _(pe):
            pe.wait_ge(ready, 1)
            n = 0
            for arr in (row0, src_f, off_f, weight):
                for b in range(0, BLOCKS, 4):
                    m = min(4, BLOCKS - b)
                    if n >= 2:
                        pe.wait_ge(taken, n - 1)
                    for j in range(m):
                        ins = pe.transpose(turned[:, n % 2, j, :], arr[:, b + j, :], k.ident[:])
                    ins.then_inc(turn, 1)
                    n += 1
            pe.wait_ge(taken, n + 1)
            pe.transpose(turned[0:1, 0, 0, :], far[:], k.ident[:]).then_inc(turn, 1)


ROW0_KIND, SRC_KIND, OFF_KIND, WEIGHT_KIND = range(4)


def relation_table(nc, k, g):
    with ExitStack() as ctx:
        a = allocator(nc, ctx)
        x = [a.sb(f"rx{i}", [P, D]) for i in range(2)]
        xn = [a.sb(f"rxn{i}", [P, D]) for i in range(2)]
        xt = [a.sb(f"rxt{i}", [P, H, P]) for i in range(2)]
        rows = [a.sb(f"rrows{i}", [P, RELS, D]) for i in range(2)]
        wblk = a.sb("wblk", [P, H, RELS, P])
        norm_ = Norm(a, k, "r")
        t_ps = [a.bank(f"rt_ps{i}", H, P) for i in range(2)]
        y_ps = [a.bank(f"ry_ps{i}", 4, P) for i in range(4)]
        wload, zeroed = a.sem("wload"), a.sem("wzeroed")
        xload = k.xload0
        s, normed, turned, taken = a.sem("rsteps"), a.sem("normed"), a.sem("rturned"), a.sem("rtaken")
        made, moved = a.sems("made", 4), a.sems("rmoved", 4)
        xfree, stored = a.sem("xfree"), a.sems("rstored", 2)
        block = ctx.enter_context(nc.Block())
        table = k.table0_d.rearrange("(r n) d -> n r d", r=RELS)
        PER = Norm.STEPS + 1

        @block.gpsimd
        def _(pool):
            pool.memset(wblk[:], 0.0).then_inc(zeroed, 1)
            pool.memset(x[0][:], 0.0).then_inc(zeroed, 1)
            pool.memset(x[1][:], 0.0).then_inc(zeroed, 1)
            pool.wait_ge(zeroed, 3)

            def load(i, par, n_rows):
                pool.wait_ge(xfree, 2 * i + par + 1)
                past_waits(pool, k)
                pool.dma_start(x[par][:n_rows, :], g["x"][cols((2 * i + par) * P, n_rows), :]
                               ).then_inc(xload[par], 16)
            node_pairs(pool, load)

        @block.sync
        def _(sp):
            sp.wait_ge(zeroed, 3)
            w = g["L0_gnn_weight"].rearrange("r (b i o) -> b i r o", i=32, o=32)
            for b in range(D // 32):
                q = 32 * (b % 4)
                sp.dma_start(wblk[q:q + 32, b // 4, :, q:q + 32], w[b]).then_inc(wload, 16)

            def store(i, par, n_rows):
                t = 2 * i + par
                for c in range(4):
                    sp.wait_ge(moved[c], t + 2)
                sp.dma_start(table[cols(t * P, P), :, :], rows[par][:]).then_inc(stored[par], 16)
            sp.sem_inc(stored[0], 16)
            sp.sem_inc(stored[1], 16)
            node_pairs(sp, store)
            sp.wait_ge(stored[0], 16 * (NODE_TILES // 2 + 2))
            sp.wait_ge(stored[1], 16 * (NODE_TILES // 2 + 1))
            sp.wait_ge(k.starts_stored, 16 * HEADS)

        @block.vector
        def _(dve):
            dve.sem_inc(xfree, 2)
            dve.wait_ge(zeroed, 3)

            def copy_chunk(i, par, c):
                t = 2 * i + par
                dve.wait_ge(stored[par], 16 * (i + 1))
                dve.wait_ge(made[c], t + 1)
                dve.tensor_copy(rows[par][:, 4 * (c % 2):4 * (c % 2) + 4, (c // 2) * P:(c // 2 + 1) * P],
                                y_ps[c]).then_inc(moved[c], 1)

            def norm(i, par, first=lambda: None, second=lambda: None):
                t = 2 * i + par
                st = Steps(dve, s, PER * t, k)
                dve.wait_ge(xload[par], 16 * (i + 1))
                dve.wait_ge(turned, t + 1)
                norm_.apply(dve, st, t, x[par][:], xn[par][:], P, first)
                dve.sem_inc(xfree, 1)
                dve.sem_inc(normed, 1)
                second()
                dve.wait_ge(turned, t + 3)
                st.then(dve.tensor_copy(xt[par][:], t_ps[par]))
                dve.sem_inc(taken, 1)

            def move(i, par, n_rows):
                if n_rows == P:
                    norm(i + par, 1 - par, lambda: copy_chunk(i, par, 0), lambda: copy_chunk(i, par, 1))
                else:
                    copy_chunk(i, par, 0)
                    copy_chunk(i, par, 1)
            norm(0, 0)
            node_pairs(dve, move)
            dve.wait_ge(s, PER * NODE_TILES)

        @block.tensor
        def _(pe):
            pe.sem_inc(turned, 2)
            pe.wait_ge(wload, 16 * (D // 32))
            for c in range(4):
                pe.sem_inc(moved[c], 1)

            def turn(t, par):
                pe.wait_ge(normed, t + 1)
                for h in range(H):
                    ins = pe.transpose(t_ps[par][:, h, :], xn[par][:, h * P:(h + 1) * P], k.ident[:])
                ins.then_inc(turned, 1)

            def mult(i, par, n_rows):
                t = 2 * i + par
                pe.wait_ge(taken, t + 1)
                for h in range(H):
                    for r in range(2):
                        c = 2 * h + r
                        pe.wait_ge(moved[c], t + 1)
                        pe.matmul(y_ps[c].rearrange("p a b -> p (a b)"), xt[par][:, h, :],
                                  wblk[:, h, 4 * r:4 * r + 4, :].rearrange("p a b -> p (a b)"),
                                  start=True, stop=True).then_inc(made[c], 1)
                    if h == 0 and n_rows == P:
                        turn(t + 1, 1 - par)
            turn(0, 0)
            node_pairs(pe, mult)

        @block.scalar
        def _(act):
            def move(i, par, n_rows):
                t = 2 * i + par
                if n_rows == P:
                    norm_.root(act, t + 1, P)
                act.wait_ge(stored[par], 16 * (i + 1))
                for c in (2, 3):
                    act.wait_ge(made[c], t + 1)
                    act.copy(rows[par][:, 4 * (c % 2):4 * (c % 2) + 4, (c // 2) * P:(c // 2 + 1) * P],
                             y_ps[c]).then_inc(moved[c], 1)
            load_tables(act, k, ACT.Sqrt)
            norm_.root(act, 0, P)
            node_pairs(act, move)


def gnn0_edges(nc, k):
    with ExitStack() as ctx:
        a = allocator(nc, ctx)
        ring = [a.sb(f"ring0_{i}", [P, D]) for i in range(2 * BT)]
        onehot = [a.sb(f"onehot0_{i}", [P, P]) for i in range(4)]
        index = [a.sb(f"index0_{i}", [P, BT], I32) for i in range(2)]
        scal = [a.sb(f"scal0_{i}", [P, 2, BT]) for i in range(2)]
        win = [a.bank(f"win0_{i}", H, P) for i in range(4)]
        got = k.got0
        hot = a.sems("hot0_", BT)
        used = a.sems("used0_", BT)
        added = a.sems("added0_", BT)
        indexed, staged = a.sem("indexed0_"), a.sem("staged0_")
        block = ctx.enter_context(nc.Block())

        @block.scalar
        def _(act):
            def stage_index(b, par):
                act.copy(index[par][:], k.meta[:, ROW0_KIND, cols(b * BT, BT)]).then_inc(indexed, 1)

            def stage_scal(b, par):
                act.copy(scal[par][:], k.meta[:, OFF_KIND:WEIGHT_KIND + 1, cols(b * BT, BT)]
                         ).then_inc(staged, 1)

            def ahead(i, par):
                b = 2 * i + par
                for t in range(BT):
                    act.wait_ge(got[par * BT + t], 16 * (i + 1))
                stage_index(b + 2, par)
                act.wait_ge(used[BT - 1], b + 3)
                stage_scal(b + 2, par)

            for par in range(2):
                stage_index(par, par)
                stage_scal(par, par)
            with act.Fori(0, BATCHES // 2) as i:
                ahead(i, 0)
                ahead(i, 1)

        @block.gpsimd
        def _(pool):
            def gather(i, par, tiles):
                b = 2 * i + par
                pool.wait_ge(indexed, b + 1)
                for t in range(tiles):
                    pool.wait_ge(used[t], b + 1)
                    past_waits(pool, k)
                    pool.indirect_dma_start(ring[par * BT + t][:], None, k.table0_d,
                                            bass.IndirectOffsetOnAxis(ap=index[par][:, t:t + 1], axis=0)
                                            ).then_inc(got[par * BT + t], 16)
            batch_pairs(pool, gather)

        @block.tensor
        def _(pe):
            for t in range(BT):
                pe.sem_inc(used[t], 2)

            def sums(i, par, tiles):
                b = 2 * i + par
                for t in range(tiles):
                    pe.wait_ge(got[par * BT + t], 16 * (i + 1))
                    pe.wait_ge(hot[t], b + 1)
                    pe.wait_ge(added[(t - 4) % BT], b + 2 if t >= 4 else b + 1)
                    for h in range(H):
                        ins = pe.matmul(win[t % 4][:, h, :], ring[par * BT + t][:, h * P:(h + 1) * P],
                                        onehot[t % 4][:], start=True, stop=True)
                    ins.then_inc(used[t], 1)
            batch_pairs(pe, sums)

        @block.vector
        def _(dve):
            for t in range(BT):
                dve.sem_inc(added[t], 1)

            def tiles_of(i, par, tiles):
                b = 2 * i + par
                dve.wait_ge(staged, b + 1)
                _, bases = nc.values_load_multi_w_load_instructions(
                    k.base[0:1, cols(b * BT + BT, tiles)], engines=[dve.engine], min_val=0, max_val=COLS - P)

                def one_hot(t):
                    dve.wait_ge(used[(t - 4) % BT], b + 3 if t >= 4 else b + 2)
                    dve.tensor_scalar(onehot[t % 4][:], k.iota[:], scal[par][:, 0, t:t + 1],
                                      scal[par][:, 1, t:t + 1], ALU.is_equal, ALU.mult).then_inc(hot[t], 1)

                one_hot(0)
                one_hot(1)
                for t in range(tiles):
                    if t + 2 < tiles:
                        one_hot(t + 2)
                    dve.wait_ge(used[t], b + 3)
                    dve.wait_ge(added[(t - 1) % BT], b + 2 if t else b + 1)
                    sums = k.acc[:, :, cols(bases[t], P)]
                    dve.tensor_tensor(sums, sums, win[t % 4][:], ALU.add).then_inc(added[t], 1)
            batch_pairs(dve, tiles_of)
            dve.wait_ge(added[LAST_TILES - 1], BATCHES + 1)


def gnn0_nodes(nc, k, g):
    with ExitStack() as ctx:
        a = allocator(nc, ctx)
        x = [a.sb(f"nx{i}", [P, D]) for i in range(2)]
        x1 = [a.sb(f"nx1_{i}", [P, D]) for i in range(2)]
        xn = [a.sb(f"nxn{i}", [P, D]) for i in range(2)]
        norm_ = Norm(a, k, "n")
        sums = [a.sb(f"nsums{i}", [P, H, P]) for i in range(2)]
        t_ps = [a.bank(f"nt_ps{i}", H, P) for i in range(2)]
        u_ps = [a.bank(f"nu_ps{i}", H, P) for i in range(2)]
        xload, stored = k.xload1, a.sems("nstored", 2)
        turned, s, normed, back, kept = (a.sem("nturned"), a.sem("nsteps"), a.sem("nnormed"),
                                         a.sem("nback"), a.sem("nkept"))
        fetched, added = a.sem("nfetched"), a.sems("nadded", 2)
        block = ctx.enter_context(nc.Block())
        PER = Norm.STEPS + 1

        @block.sync
        def _(sp):
            sp.sem_inc(stored[0], 16)
            sp.sem_inc(stored[1], 16)

            def store(i, par, rows):
                t = 2 * i + par
                sp.wait_ge(added[par], i + 1)
                sp.dma_start(k.x1_d[cols(t * P, rows), :], x1[par][:rows, :]).then_inc(stored[par], 16)
            node_pairs(sp, store)
            sp.wait_ge(stored[0], 16 * (NODE_TILES // 2 + 2))
            sp.wait_ge(stored[1], 16 * (NODE_TILES // 2 + 1))

        @block.gpsimd
        def _(pool):
            def load(i, par, rows):
                t = 2 * i + par
                pool.wait_ge(s, PER * (t + 1))
                past_waits(pool, k)
                pool.dma_start(x[par][:rows, :], g["x"][cols(t * P, rows), :]).then_inc(xload[par], 16)
            node_pairs(pool, load)

        @block.tensor
        def _(pe):
            pe.sem_inc(turned, 1)
            pe.sem_inc(back, 2)
            pe.sem_inc(kept, 2 * H)

            def turn_sums(t, par):
                pe.wait_ge(fetched, t + 1)
                for h in range(H):
                    ins = pe.transpose(t_ps[par][:, h, :], sums[par][:, h, :], k.ident[:])
                ins.then_inc(turned, 1)

            def turn(i, par, rows):
                t = 2 * i + par
                if rows == P:
                    turn_sums(t + 1, 1 - par)
                pe.wait_ge(normed, t + 1)
                pe.wait_ge(kept, H * t + H)
                for h in range(H):
                    ins = pe.transpose(u_ps[par][:, h, :rows], xn[par][:rows, h * P:(h + 1) * P],
                                       k.ident[:rows, :rows])
                ins.then_inc(back, 1)
            turn_sums(0, 0)
            node_pairs(pe, turn)

        @block.vector
        def _(dve):
            dve.sem_inc(s, 2 * PER)

            def norm(i, par, rows):
                t = 2 * i + par
                st = Steps(dve, s, PER * (t + 2), k)
                dve.wait_ge(xload[par], 16 * (i + 1))
                dve.wait_ge(turned, t + 2)
                dve.wait_ge(stored[par], 16 * (i + 1))
                st.then(dve.tensor_tensor(x1[par][:rows, :], x[par][:rows, :],
                                          t_ps[par][:rows].rearrange("p a b -> p (a b)"), ALU.add))
                dve.sem_inc(added[par], 1)
                dve.wait_ge(back, t + 1)
                norm_.apply(dve, st, t, x1[par][:rows, :], xn[par][:rows, :], rows)
                dve.sem_inc(normed, 1)
            node_pairs(dve, norm)

        @block.scalar
        def _(act):
            def fetch(t, par, rows):
                act.copy(sums[par][:, :, :rows], k.acc[:, :, cols(t * P, rows)]).then_inc(fetched, 1)

            def keep(i, par, rows):
                t = 2 * i + par
                if rows == P:
                    act.wait_ge(turned, t + 2)
                    fetch(t + 2, par, P)
                    norm_.root(act, t + 1, P)
                act.wait_ge(back, t + 3)
                for h in range(H):
                    act.activation(k.acc[:, h, cols(t * P, rows)], u_ps[par][:, h, :rows], ACT.Copy,
                                   accum_out=k.node_sums[:, h, cols(t, 1)]).then_inc(kept, 1)
            load_tables(act, k, ACT.Sqrt)
            fetch(0, 0, P)
            fetch(1, 1, P)
            norm_.root(act, 0, P)
            node_pairs(act, keep)
            act.wait_ge(kept, H * (NODE_TILES + 2))


def route(nc, k, g):
    X = EXPERTS
    with ExitStack() as ctx:
        a = allocator(nc, ctx)
        mean = a.sb("mean", [P, H])
        wr = a.sb("wr0", [P, H, X])
        br = a.sb("br0", [1, X])
        low_i = a.sb("low_i", [1, X, X], I32)
        low = a.sb("low", [1, X, X])
        num = a.sb("num", [1, X])
        v = [a.sb(f"v{i}", [1, X]) for i in range(8)]
        one = [a.sb(f"one{i}", [1, 1]) for i in range(8)]
        m = [a.sb(f"m{i}", [1, X, X]) for i in range(3)]
        top = a.sb("top", [1, 2])
        pick = a.sb("pick", [1, 2])
        pick_i = a.sb("pick_i", [1, 2], I32)
        tw = a.sb("tw", [1, 2])
        bcast = a.sb("bcast", [P, 2])
        b2 = a.sb("b2_2", [1, 2, D])
        b2s = a.sb("b2s", [1, 2, D])
        lg_ps = a.bank("lg_ps", X)
        w_ps = a.bank("w_ps", 2)
        small, made, s, to_pe, pe_done, to_act, act_done, picked, wload = (
            a.sem(f"route_{n}") for n in ("small", "made", "s", "to_pe", "pe", "to_act", "act", "picked", "w"))
        block = ctx.enter_context(nc.Block())

        @block.gpsimd
        def _(pool):
            pool.iota(low_i[:], [[1, X], [-1, X]], base=0, channel_multiplier=0).then_inc(made, 1)

        @block.sync
        def _(sp):
            sp.dma_start(wr[:], g["L0_ffn_Wr"].rearrange("(h p) x -> p h x", p=P)).then_inc(small, 16)
            sp.dma_start(br[:], g["L0_ffn_br"].rearrange("(a x) -> a x", a=1)).then_inc(small, 16)
            sp.wait_ge(picked, 1)
            _, which = nc.values_load_multi_w_load_instructions(
                pick_i[0:1, 0:2], engines=[sp.engine], min_val=0, max_val=X - 1)
            with nc.allow_non_contiguous_dma(reason="biases onto partitions"):
                for j in range(2):
                    sp.dma_start(k.w1[:, j, :, :], g["L0_ffn_W1"][cols(which[j], 1), :, :].rearrange(
                        "x (h p) f -> p (x h) f", p=P)).then_inc(wload, 16)
                    sp.dma_start(k.w2[:, j, :, :], g["L0_ffn_W2"][cols(which[j], 1), :, :].rearrange(
                        "x (c p) d -> p (x c) d", p=P)).then_inc(wload, 16)
                    sp.dma_start(k.b1[:, j, :], g["L0_ffn_b1"][cols(which[j], 1), :].rearrange(
                        "x (c p) -> p (x c)", p=P)).then_inc(wload, 16)
                    sp.dma_start(b2[:, j, :], g["L0_ffn_b2"][cols(which[j], 1), :]).then_inc(wload, 16)
            sp.wait_ge(wload, 128)

        @block.tensor
        def _(pe):
            pe.wait_ge(small, 32)
            pe.wait_ge(to_pe, 1)
            for h in range(H):
                ins = pe.matmul(lg_ps[0:1, :], mean[:, h:h + 1], wr[:, h, :], start=(h == 0), stop=(h == H - 1))
            ins.then_inc(pe_done, 1)
            pe.wait_ge(to_pe, 2)
            pe.matmul(w_ps, k.ones[0:1, :], tw[:], start=True, stop=True).then_inc(pe_done, 1)

        @block.scalar
        def _(act):
            act.wait_ge(to_act, 1)
            act.activation(v[1][:], v[0][:], ACT.Exp, bias=one[0][:], accum_out=one[1][:]).then_inc(act_done, 1)
            act.wait_ge(to_act, 2)
            act.activation(v[6][:], v[5][:], ACT.Exp, bias=one[3][:], accum_out=one[4][:]).then_inc(act_done, 1)
            act.wait_ge(to_act, 3)
            act.activation(one[6][:], one[5][:], ACT.Exp).then_inc(act_done, 1)

        @block.vector
        def _(dve):
            st = Steps(dve, s, 0, k)
            dve.wait_ge(made, 1)
            st.then(dve.tensor_copy(low[:], low_i[:]))
            st.then(dve.tensor_copy(num[:], low[:, :, 0]))
            st.then(dve.tensor_scalar(low[:], low[:], 0.0, None, ALU.is_gt))
            st.then(dve.tensor_reduce(mean[:], k.node_sums[:], AX, ALU.add))
            st.then(dve.tensor_scalar(mean[:], mean[:], 1.0 / N, None, ALU.mult))
            dve.sem_inc(to_pe, 1)
            dve.wait_ge(pe_done, 1)
            st.then(dve.tensor_tensor(v[0][:], lg_ps[0:1, :], br[:], ALU.add))
            st.then(dve.tensor_reduce(one[0][:], v[0][:], AX, ALU.max, negate=True))
            dve.sem_inc(to_act, 1)
            dve.wait_ge(act_done, 1)
            st.then(dve.reciprocal(one[1][:], one[1][:]))
            st.then(dve.tensor_scalar(v[2][:], v[1][:], one[1][:], None, ALU.mult))
            st.then(dve.tensor_scalar(v[3][:], v[2][:], float(N), 1e-30, ALU.mult, ALU.max))
            st.then(dve.reciprocal(v[4][:], v[3][:]))
            st.then(dve.tensor_scalar(v[4][:], v[4][:], CAPACITY, 1.0, ALU.mult, ALU.min))
            st.then(dve.tensor_tensor(v[5][:], v[2][:], v[4][:], ALU.mult))
            st.then(dve.tensor_reduce(one[3][:], v[5][:], AX, ALU.max, negate=True))
            dve.sem_inc(to_act, 1)
            dve.wait_ge(act_done, 2)
            st.then(dve.reciprocal(one[4][:], one[4][:]))
            st.then(dve.tensor_scalar(v[6][:], v[6][:], one[4][:], None, ALU.mult))
            zi = v[6][:].unsqueeze(2).broadcast_to([1, X, X])
            zj = v[6][:].unsqueeze(1).broadcast_to([1, X, X])
            st.done(dve.tensor_tensor(m[0][:], zj, zi, ALU.is_gt))
            st.then(dve.tensor_tensor(m[1][:], zj, zi, ALU.is_equal))
            st.then(dve.tensor_tensor(m[1][:], m[1][:], low[:], ALU.mult))
            st.then(dve.tensor_tensor(m[0][:], m[0][:], m[1][:], ALU.add))
            st.then(dve.tensor_reduce(v[7][:], m[0][:], AX, ALU.add))
            for j in range(2):
                st.then(dve.tensor_scalar(v[0][:], v[7][:], float(j), None, ALU.is_equal))
                st.then(dve.tensor_tensor(v[1][:], v[0][:], num[:], ALU.mult))
                st.then(dve.tensor_reduce(pick[:, j:j + 1], v[1][:], AX, ALU.add))
                st.then(dve.tensor_tensor(v[1][:], v[0][:], v[6][:], ALU.mult))
                st.then(dve.tensor_reduce(top[:, j:j + 1], v[1][:], AX, ALU.add))
            st.then(dve.tensor_copy(pick_i[:], pick[:]))
            dve.sem_inc(picked, 1)
            st.then(dve.tensor_tensor(one[5][:], top[:, 1:2], top[:, 0:1], ALU.subtract))
            dve.sem_inc(to_act, 1)
            dve.wait_ge(act_done, 3)
            st.then(dve.tensor_scalar(one[7][:], one[6][:], 1.0, None, ALU.add))
            st.then(dve.reciprocal(tw[:, 0:1], one[7][:]))
            st.then(dve.tensor_tensor(tw[:, 1:2], one[6][:], tw[:, 0:1], ALU.mult))
            dve.sem_inc(to_pe, 1)
            dve.wait_ge(pe_done, 2)
            st.then(dve.tensor_copy(bcast[:], w_ps))
            dve.wait_ge(wload, 128)
            for j in range(2):
                st.done(dve.tensor_scalar(k.w2[:, j, :, :], k.w2[:, j, :, :], bcast[:, j:j + 1], None, ALU.mult))
                st.done(dve.tensor_scalar(b2s[:, j, :], b2[:, j, :], tw[:, j:j + 1], None, ALU.mult))
            st.wait()
            st.then(dve.tensor_tensor(k.b2[:], b2s[:, 0, :], b2s[:, 1, :], ALU.add))


def tiles(gi):
    return [LAST_ROWS] if isinstance(gi, int) and gi == GROUPS else [P] * GROUP


def groups(eng, emit, first=0, last=GROUPS - 1):
    with eng.Fori(first, last + 1) as i:
        emit(i)


def group_norms(dve, st, k, x, b, sizes):
    r, n = sizes[0], len(sizes)
    past_waits(dve, k)
    for t in range(n):
        st.done(dve.bn_stats(b.stats[:r, t, :], x[:r, t, :]))
    st.wait()
    past_waits(dve, k)
    for t in range(n):
        st.done(dve.bn_aggr(b.mv[:r, t, :], b.stats[:r, t, :]))
    st.wait()
    st.then(dve.tensor_scalar(b.var[:r, 0:n], b.mv[:r, 0:n, 1], LN_EPS, None, ALU.add))
    inverse_root(dve, st, b.var[:r, 0:n], b.rstd[:r, 0:n], b.tmp[:r, 0:n])


GROUP_NORM_STEPS = 2 * GROUP + 1 + INVERSE_ROOT_STEPS


def ffn0(nc, k, g):
    C = 2 * F0 // P
    with ExitStack() as ctx:
        a = allocator(nc, ctx)
        hid = a.sb("hid", [P, C, GCOLS])
        xg = a.sb("xg", [P, H, GCOLS])
        x1, y, x2, xn2 = (a.sb(f"f{n}", [P, GROUP, D]) for n in ("x1", "y", "x2", "xn2"))
        xt = a.sb("fxt", [P, H, P])
        row = a.sb("frow", [P, 2, ROW1])
        prod = a.sb("fprod", [P, D])
        gamma, beta, asrc = (a.sb(n, [P, D]) for n in ("gamma", "beta", "asrc"))
        wp = a.sb("wp", [P, H, D])
        b2_t = a.sb("b2_t", [P, H])
        ln = Named()
        ln.stats, ln.mv = a.sb("fstats", [P, GROUP, 6]), a.sb("fmv", [P, GROUP, 2])
        ln.var, ln.rstd, ln.tmp = (a.sb(f"f{n}", [P, GROUP]) for n in ("var", "rstd", "tmp"))
        h_ps = [a.bank(f"fh_ps{i}", GCOLS) for i in range(2)]
        y_ps = [a.bank(f"fy_ps{i}", D) for i in range(2)]
        t_ps = a.bank("ft_ps", H, P)
        p_ps = a.bank("fp_ps", D)
        small, x_load, x_ready = a.sem("fsmall"), a.sem("fx_load"), a.sem("fx_ready")
        b2_made, b2_kept, xg_made = a.sem("b2_made"), a.sem("b2_kept"), a.sem("xg_made")
        h_made, h_kept = a.sem("h_made"), a.sem("h_kept")
        y_made, y_moved = a.sem("y_made"), a.sem("y_moved")
        s, row_steps = a.sem("fsteps"), a.sem("row_steps")
        y_free, x2_done, normed = a.sem("y_free"), a.sem("x2_done"), a.sem("fnormed")
        x2_stored = a.sem("x2_stored")
        turned, t_kept, p_made, p_moved, row_done = (
            a.sem(f"f_{n}") for n in ("turned", "t_kept", "p_made", "p_moved", "row_done"))
        row_stored = a.sems("row_stored", 2)
        block = ctx.enter_context(nc.Block())

        def all_groups(eng, head=None, main=None, project=None, turn=None, end=None):
            def do(gi, mine, tail):
                if head and mine:
                    head(gi)
                for t in range(max(len(mine), len(tail)) + 1):
                    if main and t < len(mine):
                        main(gi, t, mine[t])
                    if project and 1 <= t <= len(tail):
                        project(gi - 1, t - 1, tail[t - 1])
                    if turn and t < len(tail):
                        turn(gi - 1, t, tail[t])
                if end and mine:
                    end(gi)
            do(0, tiles(0), [])
            groups(eng, lambda gi: do(gi, tiles(gi), tiles(gi - 1)), 1)
            do(GROUPS, tiles(GROUPS), tiles(GROUPS - 1))
            do(GROUPS + 1, [], tiles(GROUPS))

        @block.sync
        def _(sp):
            for t, name in ((gamma, "L0_ffn_gamma"), (beta, "L0_ffn_beta")):
                sp.dma_start(t[:], g[name].rearrange("(a d) -> a d", a=1).broadcast_to([P, D])).then_inc(small, 16)
            sp.dma_start(asrc[:], g["L1_gnn_a_src"].rearrange("(a h) d -> a (h d)", a=1).broadcast_to([P, D])
                         ).then_inc(small, 16)
            sp.dma_start(wp[:], g["L1_gnn_W"].rearrange("(h p) d -> p h d", p=P)).then_inc(small, 16)
            sp.sem_inc(y_free, 1)
            sp.sem_inc(x2_stored, 16)
            sp.sem_inc(row_stored[0], 16)
            sp.sem_inc(row_stored[1], 16)

            def rows_of(dram, t, gi, sizes):
                if len(sizes) == GROUP:
                    return dram[cols(gi * GCOLS, GCOLS), :].rearrange("(t p) d -> p t d", p=P), t[:]
                return dram[gi * GCOLS:N, :], t[:sizes[0], 0, :]

            def load(gi):
                sp.wait_ge(y_free, gi + 1)
                src, dst = rows_of(k.x1_d, x1, gi, tiles(gi))
                sp.dma_start(dst, src).then_inc(x_load, 16)

            def store_x2(gi):
                sp.wait_ge(x2_done, gi + 1)
                dst, src = rows_of(k.x2_d, x2, gi, tiles(gi))
                sp.dma_start(dst, src).then_inc(x2_stored, 16)

            def store_row(gi, t, r):
                n = GROUP * gi + t
                sp.wait_ge(row_done, n + 1)
                sp.dma_start(k.table1_d[cols(n * P, r), :], row[:r, t % 2, :]).then_inc(row_stored[t % 2], 16)

            all_groups(sp, head=load, project=store_row, end=store_x2)
            sp.wait_ge(x2_stored, 16 * (GROUPS + 2))
            sp.wait_ge(row_stored[0], 16 * (2 * GROUPS + 2))
            sp.wait_ge(row_stored[1], 16 * (2 * GROUPS + 1))

        @block.gpsimd
        def _(pool):
            pool.wait_ge(small, 64)

            def add_beta(gi):
                r, n = tiles(gi)[0], len(tiles(gi))
                pool.wait_ge(x_load, 16 * gi + 16)
                pool.tensor_tensor(x1[:r, 0:n, :], x1[:r, 0:n, :], beta[:r, :].unsqueeze(1).broadcast_to([r, n, D]),
                                   ALU.add).then_inc(x_ready, 1)
            all_groups(pool, head=add_beta)

        @block.tensor
        def _(pe):
            pe.sem_inc(h_kept, 2)
            pe.sem_inc(p_moved, 1)
            pe.sem_inc(y_moved, 2)
            for h in range(H):
                ins = pe.matmul(p_ps[:, h:h + 1], k.b2[0:1, h * P:(h + 1) * P], k.ones[0:1, 0:1],
                                start=True, stop=True)
            ins.then_inc(b2_made, 1)
            pe.wait_ge(small, 64)

            def hidden(gi):
                n = sum(tiles(gi))
                for c in range(C):
                    j, f = c // (C // 2), c % (C // 2)
                    pe.wait_ge(h_kept, C * gi + c + 1)
                    for h in range(H):
                        rhs = k.acc[:, h, cols(gi * GCOLS, n)]
                        ins = pe.matmul(h_ps[c % 2][:, :n], k.w1[:, j, h, f * P:(f + 1) * P], rhs,
                                        start=(h == 0), stop=(h == H - 1))
                    ins.then_inc(h_made, 1)

            def output(gi, t, r):
                pe.wait_ge(y_moved, GROUP * gi + t + 1)
                yb = y_ps[t % 2]
                if t == 0:
                    pe.wait_ge(xg_made, gi + 1)
                for h in range(H):
                    pe.matmul(yb[:r, h * P:(h + 1) * P], xg[:, h, t * P:t * P + r], k.ident[:],
                              start=(h == 0), stop=False, skip_group_check=True)
                for c in range(C):
                    if t == 0:
                        pe.wait_ge(h_kept, C * gi + c + 3)
                    ins = pe.matmul(yb[:r, 0:D], hid[:, c, t * P:t * P + r], k.w2[:, c // 4, c % 4, :],
                                    start=False, stop=(c == C - 1), skip_group_check=True)
                ins.then_inc(y_made, 1)

            def turn(gi, t, r):
                pe.wait_ge(normed, gi + 1)
                for h in range(H):
                    ins = pe.transpose(t_ps[:, h, :r], xn2[:r, t, h * P:(h + 1) * P], k.ident[:r, :r])
                ins.then_inc(turned, 1)

            def project(gi, t, r):
                pe.wait_ge(t_kept, GROUP * gi + t + 1)
                pe.wait_ge(p_moved, GROUP * gi + t + 1)
                for h in range(H):
                    ins = pe.matmul(p_ps[:r, 0:D], xt[:, h, :r], wp[:, h, :], start=(h == 0), stop=(h == H - 1))
                ins.then_inc(p_made, 1)

            all_groups(pe, head=hidden, main=output, project=project, turn=turn)

        @block.scalar
        def _(act):
            act.wait_ge(b2_made, 1)
            act.copy(b2_t[:], p_ps[:, 0:H]).then_inc(b2_kept, 1)
            act.wait_ge(b2_kept, 1)
            load_tables(act, k, ACT.Gelu)

            def keep(gi):
                n = sum(tiles(gi))
                act.wait_ge(h_made, C * gi + 1)
                if not (isinstance(gi, int) and gi == 0):
                    act.wait_ge(y_made, GROUP * gi)
                for h in range(H):
                    ins = act.activation(xg[:, h, :n], k.acc[:, h, cols(gi * GCOLS, n)], ACT.Identity,
                                         bias=b2_t[:, h:h + 1])
                ins.then_inc(xg_made, 1)
                for c in range(C):
                    act.wait_ge(h_made, C * gi + c + 1)
                    act.activation(hid[:, c, :n], h_ps[c % 2][:, :n], ACT.Gelu,
                                   bias=k.b1[:, c // 4, c % 4:c % 4 + 1]).then_inc(h_kept, 1)

            def move_y(gi, t, r):
                if t == 0:
                    act.wait_ge(y_free, gi + 1)
                act.wait_ge(y_made, GROUP * gi + t + 1)
                act.copy(y[:r, t, :], y_ps[t % 2][:r, 0:D]).then_inc(y_moved, 1)

            def keep_turned(gi, t, r):
                act.wait_ge(turned, GROUP * gi + t + 1)
                act.copy(xt[:, :, :r], t_ps[:, 0:H, :r]).then_inc(t_kept, 1)

            def move_row(gi, t, r):
                act.wait_ge(p_made, GROUP * gi + t + 1)
                act.wait_ge(row_stored[t % 2], 16 * (2 * gi + t // 2 + 1))
                act.copy(row[:r, t % 2, 0:D], p_ps[:r, 0:D]).then_inc(p_moved, 1)
            all_groups(act, head=keep, main=move_y, project=move_row, turn=keep_turned)

        @block.vector
        def _(dve):
            dve.wait_ge(small, 64)
            NPER, RPER = 2 * GROUP_NORM_STEPS + 3 * GROUP, 2

            def norms(gi):
                sizes = tiles(gi)
                r, n = sizes[0], len(sizes)
                st = Steps(dve, s, NPER * gi, k)
                dve.wait_ge(y_moved, GROUP * gi + n + 2)
                group_norms(dve, st, k, y, ln, sizes)
                for t in range(n):
                    st.done(dve.scalar_tensor_tensor(y[:r, t, :], y[:r, t, :], ln.mv[:r, t, 0:1], gamma[:r, :],
                                                     ALU.subtract, ALU.mult))
                st.wait()
                dve.wait_ge(x_ready, gi + 1)
                dve.wait_ge(x2_stored, 16 * gi + 16)
                for t in range(n):
                    st.done(dve.scalar_tensor_tensor(x2[:r, t, :], y[:r, t, :], ln.rstd[:r, t:t + 1], x1[:r, t, :],
                                                     ALU.mult, ALU.add))
                st.wait()
                dve.sem_inc(y_free, 1)
                dve.sem_inc(x2_done, 1)
                group_norms(dve, st, k, x2, ln, sizes)
                for t in range(n):
                    st.done(dve.tensor_scalar(xn2[:r, t, :], x2[:r, t, :], ln.mv[:r, t, 0:1], ln.rstd[:r, t:t + 1],
                                              ALU.subtract, ALU.mult))
                st.wait()
                assert n < GROUP or st.n == NPER
                dve.sem_inc(normed, 1)

            def scores(gi, t, r):
                n = GROUP * gi + t
                st = Steps(dve, row_steps, RPER * n, k)
                dve.wait_ge(p_moved, n + 2)
                st.then(dve.tensor_tensor(prod[:r, :], row[:r, t % 2, 0:D], asrc[:r, :], ALU.mult))
                st.then(dve.tensor_reduce(row[:r, t % 2, D:ROW1], prod[:r, :].rearrange(
                    "p (h d) -> p h d", h=HEADS), AX, ALU.add))
                assert st.n == RPER
                dve.sem_inc(row_done, 1)

            all_groups(dve, project=scores, end=norms)


def gnn1_edges(nc, k):
    with ExitStack() as ctx:
        a = allocator(nc, ctx)
        ring = a.sb("ring1", [P, 2 * BT, ROW1])
        onehot = a.sb("onehot1", [P, 2, BT, P])
        index = [a.sb(f"index1_{i}", [P, BT], I32) for i in range(2)]
        off = [a.sb(f"off1_{i}", [P, BT]) for i in range(2)]
        starts = [a.sb(f"starts1_{i}", [P, P + 1]) for i in range(2)]
        alpha = a.sb("alpha", [P, BT * HEADS])
        local = a.sb("local", [P, 2 * P])
        spread = a.sb("spread", [P, 2, BT])
        chain = a.sb("chain", [HEADS, 2 * BT + 1])
        joined, ends = a.sb("joined", [HEADS, 2 * BT + 1]), a.sb("ends1", [HEADS, 2 * BT + 1])
        picked = a.sb("picked", [P, 2, BT])
        edge_max = a.sb("edge_max", [P, 2])
        m1, m2 = a.sb("max_forth", [P, P]), a.sb("max_back", [P, P])
        prob = a.sb("prob", [P, BT * HEADS])
        gap, fade = a.sb("gap", [HEADS, 1]), a.sb("fade", [HEADS, 1])
        nodes = a.sb("nodes", [P, ROW1])
        win = [a.bank(f"win1_{i}", 3, P) for i in range(4)]
        batch_win, win_turned = win[0].rearrange("p a b -> p (a b)")[:, 0:ROW1], win[1]
        a_ps, small_ps, p_ps = a.bank("a_ps", P), a.bank("small_ps", 2, P), a.bank("p_ps", P)
        fade_ps = a.bank("fade_ps", H)
        got = k.got1
        hot = a.sems("hot1_", BT)
        used = a.sems("used1_", BT)
        added = a.sems("added1_", BT)
        indexed, staged = a.sem("indexed1_"), a.sem("staged1_")
        st_load, zeroed = a.sems("st_load", 2), a.sem("zeroed1")
        weighted, moved, turned_back = a.sem("g1_weighted"), a.sem("g1_moved"), a.sem("g1_turned_back")
        alpha_c, a_turned, s, to_pe, pe_small, p_turned, p_done, gap_made, fade_made = (
            a.sem(f"g1_{n}") for n in ("alpha", "aturn", "steps", "to_pe", "pe_small", "pturn", "pdone", "gap", "fade"))
        block = ctx.enter_context(nc.Block())
        QUAD = 4

        assert LAST_TILES % QUAD == 0 and LAST_TILES < BT

        def either(eng, narrow, general):
            _, flag = nc.values_load_multi_w_load_instructions(k.narrow[:], engines=[eng.engine],
                                                               min_val=0, max_val=1)
            with eng.If(flag[0] == 1):
                batch_pairs(eng, narrow)
            with eng.Else():
                batch_pairs(eng, general)

        @block.sync
        def _(sp):
            def load(i, par, tiles):
                b = 2 * i + par
                sp.wait_ge(p_done, b + 1)
                sp.dma_start(starts[par][:], k.starts_d[:, cols(b * BT, BT), :]).then_inc(st_load[par], 16)
            batch_pairs(sp, load)

        @block.gpsimd
        def _(pool):
            def gather(i, par, tiles):
                b = 2 * i + par
                pool.wait_ge(indexed, b + 1)
                for t in range(tiles):
                    pool.wait_ge(used[t], b + 1)
                    past_waits(pool, k)
                    pool.indirect_dma_start(ring[:, par * BT + t, :], None, k.table1_d,
                                            bass.IndirectOffsetOnAxis(ap=index[par][:, t:t + 1], axis=0)
                                            ).then_inc(got[par * BT + t], 16)
            batch_pairs(pool, gather)

        @block.scalar
        def _(act):
            act.sem_inc(p_done, 2)
            load_tables(act, k, ACT.Exp)

            def stage_index(b, par):
                act.copy(index[par][:], k.meta[:, SRC_KIND, cols(b * BT, BT)]).then_inc(indexed, 1)

            def stage_off(b, par):
                act.copy(off[par][:], k.meta[:, OFF_KIND, cols(b * BT, BT)]).then_inc(staged, 1)

            def scores(i, par, tiles, between=lambda: None):
                b = 2 * i + par
                for t in range(tiles):
                    act.wait_ge(got[par * BT + t], 16 * (i + 1))
                act.wait_ge(a_turned, b + 1)
                act.copy(alpha[:].rearrange("p (h t) -> p t h", h=HEADS),
                         ring[:, par * BT:(par + 1) * BT, D:ROW1]).then_inc(alpha_c, 1)
                if tiles == BT:
                    stage_index(b + 2, par)
                between()
                act.wait_ge(gap_made, b + 1)
                act.activation(fade[:], gap[:], ACT.Exp).then_inc(fade_made, 1)
                act.wait_ge(p_turned, b + 1)

            def move_window(m, last_tile):
                act.wait_ge(used[last_tile], m + 2)
                act.copy(nodes[:], batch_win).then_inc(moved, 1)

            def narrow(i, par, tiles):
                b = 2 * i + par
                scores(i, par, tiles, lambda: move_window(b, BT - 1))
                act.activation(ring[:, par * BT:(par + 1) * BT, D:ROW1], p_ps.rearrange(
                    "p (h t) -> p t h", h=HEADS), ACT.Exp).then_inc(p_done, 1)
                if tiles == LAST_TILES:
                    move_window(b + 1, LAST_TILES - 1)

            def general(i, par, tiles):
                b = 2 * i + par
                scores(i, par, tiles)
                act.wait_ge(used[BT - 1], b + 2)
                act.activation(prob[:], p_ps, ACT.Exp).then_inc(p_done, 1)
                if tiles == BT:
                    if par == 0:
                        act.wait_ge(used[BT - 1], b + 2)
                    stage_off(b + 1, 1 - par)

            stage_index(0, 0)
            stage_index(1, 1)
            stage_off(0, 0)
            act.wait_ge(zeroed, 5)
            either(act, narrow, general)

        @block.tensor
        def _(pe):
            for t in range(BT):
                pe.sem_inc(used[t], 2)
            pe.sem_inc(a_turned, 1)

            def scores(b, between=lambda: None):
                pe.wait_ge(alpha_c, b + 1)
                pe.wait_ge(p_done, b + 2)
                pe.transpose(a_ps, alpha[:], k.ident[:]).then_inc(a_turned, 1)
                between()
                pe.wait_ge(to_pe, 3 * b + 1)
                pe.matmul(small_ps[0:HEADS, 0, 0:2 * BT], k.head_of[:], spread[:].rearrange("p a b -> p (a b)"),
                          start=True, stop=True).then_inc(pe_small, 1)
                pe.wait_ge(to_pe, 3 * b + 2)
                pe.matmul(small_ps[:, 1, 0:2 * BT + 1], k.head_of_t[:], joined[:], start=True, stop=True
                          ).then_inc(pe_small, 1)
                pe.wait_ge(to_pe, 3 * b + 3)
                pe.transpose(p_ps, m1[:], k.ident[:]).then_inc(p_turned, 1)
                pe.wait_ge(fade_made, b + 1)
                for h in range(H):
                    ins = pe.matmul(fade_ps[:, h:h + 1], k.head_rows[:, h * P:(h + 1) * P], fade[:],
                                    start=True, stop=True)
                ins.then_inc(pe_small, 1)

            def turn_back(m):
                pe.wait_ge(moved, m + 1)
                for h in range(H):
                    pe.transpose(win_turned[:, h, :], nodes[:, h * P:(h + 1) * P], k.ident[:])
                pe.transpose(win_turned[0:HEADS, 2, :], nodes[:, D:ROW1], k.ident[:]).then_inc(turned_back, 1)

            def narrow(i, par, tiles):
                b = 2 * i + par
                scores(b, lambda: turn_back(b))
                for t in range(tiles):
                    if t % QUAD == 0:
                        pe.wait_ge(weighted, BT // QUAD * b + t // QUAD + 1)
                    pe.matmul(batch_win, onehot[:, par, t, :], ring[:, par * BT + t, :],
                              start=(t == 0), stop=(t == tiles - 1)).then_inc(used[t], 1)
                if tiles == LAST_TILES:
                    turn_back(b + 1)

            def general(i, par, tiles):
                b = 2 * i + par
                scores(b)
                for t in range(tiles):
                    pe.wait_ge(hot[t], 2 * b + 2)
                    pe.wait_ge(added[(t - 4) % BT], b + 2 if t >= 4 else b + 1)
                    slot, hot_t = ring[:, par * BT + t, :], onehot[:, 0, t % 4, :]
                    for h in range(H):
                        pe.matmul(win[t % 4][:, h, :], slot[:, h * P:(h + 1) * P], hot_t,
                                  start=True, stop=True)
                    pe.matmul(win[t % 4][0:HEADS, 2, :], prob[:, t:BT * HEADS:BT], hot_t,
                              start=True, stop=True).then_inc(used[t], 1)
            either(pe, narrow, general)

        @block.vector
        def _(dve):
            for t in range(BT):
                dve.sem_inc(added[t], 1)
            st0 = Steps(dve, zeroed, 0, k)
            st0.done(dve.memset(chain[:], -BIG))
            st0.then(dve.memset(k.acc_s[:], 0.0))
            st0.done(dve.memset(k.acc[:, 0, :], 0.0))
            st0.then(dve.memset(k.acc[:, 1, :], 0.0))
            st0.then(dve.memset(batch_win, 0.0))
            SCORES = 15
            FADES = 2

            def scores(b, i, par, st, between=lambda: None):
                before = st.n
                fl = starts[par]
                st.done(dve.tensor_copy(ends[:], k.ends8[:, cols(2 * BT * b, 2 * BT + 1)]))
                dve.wait_ge(a_turned, b + 2)
                dve.wait_ge(st_load[par], 16 * (i + 1))
                st.then(dve.tensor_tensor_scan(local[:, 0:P], fl[:, 0:P], a_ps, -BIG, ALU.add, ALU.max))
                st.then(dve.tensor_tensor_scan(local[:, P:2 * P][:, ::-1], fl[:, 1:P + 1][:, ::-1],
                                               local[:, 0:P][:, ::-1], -BIG, ALU.add, ALU.max))
                st.then(dve.tensor_tensor(spread[:], k.tile_of[:].unsqueeze(1).broadcast_to([P, 2, BT]),
                                          local[:, P - 1:P + 1].unsqueeze(2).broadcast_to([P, 2, BT]), ALU.mult))
                dve.sem_inc(to_pe, 1)
                between()
                dve.wait_ge(pe_small, 3 * b + 1)
                lastfirst = small_ps[0:HEADS, 0, 0:2 * BT]
                st.done(dve.tensor_tensor_scan(chain[:, 2:2 * BT + 1:2], k.both8[:, cols(BT * b, BT)],
                                               lastfirst[:, 0:BT], chain[:, 0:1], ALU.add, ALU.max))
                st.then(dve.tensor_copy(chain[:, 1:2 * BT:2], lastfirst[:, BT:2 * BT]))
                st.then(dve.tensor_tensor_scan(joined[:, ::-1], ends[:, ::-1], chain[:, ::-1], -BIG,
                                               ALU.add, ALU.max))
                dve.sem_inc(to_pe, 1)
                st.then(dve.tensor_tensor(gap[:], chain[:, 0:1], joined[:, 0:1], ALU.subtract))
                dve.sem_inc(gap_made, 1)
                st.then(dve.tensor_copy(chain[:, 0:1], chain[:, 2 * BT:2 * BT + 1]))
                dve.wait_ge(pe_small, 3 * b + 2)
                for j in range(2):
                    st.done(dve.tensor_tensor(picked[:, j, :], small_ps[:, 1, 2 * j:2 * (BT + j) - 1:2],
                                              k.tile_of[:], ALU.mult))
                st.wait()
                st.then(dve.tensor_reduce(edge_max[:], picked[:], AX, ALU.add))
                st.then(dve.tensor_tensor_scan(m1[:], fl[:, 0:P], local[:, P:2 * P], edge_max[:, 0:1],
                                               ALU.add, ALU.max))
                st.then(dve.tensor_tensor_scan(m2[:, ::-1], fl[:, 1:P + 1][:, ::-1], m1[:, ::-1],
                                               edge_max[:, 1:2], ALU.add, ALU.max))
                st.then(dve.tensor_tensor(m1[:], a_ps, m2[:], ALU.subtract))
                dve.sem_inc(to_pe, 1)
                assert st.n - before in (SCORES, SCORES + 2)

            def fade_open(b, base, st):
                dve.wait_ge(pe_small, 3 * b + 3)
                one, one_s = k.acc[:, :, cols(base, 1)], k.acc_s[:, cols(base, 1)]
                st.done(dve.tensor_tensor(one, one, fade_ps.unsqueeze(2), ALU.mult))
                st.then(dve.tensor_tensor(one_s, one_s, fade[:], ALU.mult))

            def base_of(m):
                _, base = nc.values_load_multi_w_load_instructions(
                    k.base[0:1, cols(m * BT, 1)], engines=[dve.engine], min_val=0, max_val=COLS - P)
                return base[0]

            def add_window(m, base, st):
                dve.wait_ge(turned_back, m + 1)
                sums, sums_s = k.acc[:, :, cols(base, P)], k.acc_s[:, cols(base, P)]
                st.done(dve.tensor_tensor(sums, sums, win_turned[:, 0:H, :], ALU.add))
                st.then(dve.tensor_tensor(sums_s, sums_s, win_turned[0:HEADS, 2, :], ALU.add))

            def narrow(i, par, tiles):
                b = 2 * i + par
                st = Steps(dve, s, (SCORES + FADES + 3) * b, k)
                past_waits(dve, k)
                base_before, base = base_of(b), base_of(b + 1)
                for t in range(0, tiles, QUAD):
                    ins = dve.tensor_tensor(
                        onehot[:, par, t:t + QUAD, :], k.iota[:].unsqueeze(1).broadcast_to([P, QUAD, P]),
                        k.near[:, cols(b * BT + t, QUAD)].unsqueeze(2).broadcast_to([P, QUAD, P]), ALU.is_equal)
                st.done(ins)
                scores(b, i, par, st, lambda: add_window(b, base_before, st))
                dve.wait_ge(p_done, b + 3)
                for t in range(0, tiles, QUAD):
                    quad = ring[:, par * BT + t:par * BT + t + QUAD, :]
                    rows = quad[:, :, 0:D].rearrange("p t (h d) -> p t h d", h=HEADS)
                    dve.tensor_tensor(rows, rows, quad[:, :, D:ROW1].unsqueeze(3).broadcast_to(
                        [P, QUAD, HEADS, HD]), ALU.mult).then_inc(weighted, 1)
                fade_open(b, base, st)
                if tiles == LAST_TILES:
                    add_window(b + 1, base, st)

            def general(i, par, tiles):
                b = 2 * i + par
                st = Steps(dve, s, (SCORES + FADES) * b, k)
                scores(b, i, par, st)
                _, bases = nc.values_load_multi_w_load_instructions(
                    k.base[0:1, cols(b * BT + BT, tiles)], engines=[dve.engine], min_val=0, max_val=COLS - P)
                dve.wait_ge(added[BT - 1], b + 1)
                fade_open(b, bases[0], st)

                def one_hot(t):
                    dve.wait_ge(used[(t - 4) % BT], b + 3 if t >= 4 else b + 2)
                    dve.tensor_scalar(onehot[:, 0, t % 4, :], k.iota[:], off[par][:, t:t + 1], None, ALU.is_equal
                                      ).then_inc(hot[t], 1)
                    rows = ring[:, par * BT + t, 0:D].rearrange("p (h d) -> p h d", h=HEADS)
                    dve.tensor_tensor(rows, rows, prob[:, t:BT * HEADS:BT].unsqueeze(2).broadcast_to(
                        [P, HEADS, HD]), ALU.mult).then_inc(hot[t], 1)

                dve.wait_ge(p_done, b + 3)
                dve.wait_ge(staged, b + 1)
                one_hot(0)
                one_hot(1)
                for t in range(tiles):
                    if t + 2 < tiles:
                        one_hot(t + 2)
                    dve.wait_ge(used[t], b + 3)
                    dve.wait_ge(added[(t - 1) % BT], b + 2 if t else b + 1)
                    sums = k.acc[:, :, cols(bases[t], P)]
                    sums_s = k.acc_s[:, cols(bases[t], P)]
                    dve.tensor_tensor(sums_s, sums_s, win[t % 4][0:HEADS, 2, :], ALU.add)
                    dve.tensor_tensor(sums, sums, win[t % 4][:, 0:H, :], ALU.add).then_inc(added[t], 1)
                if tiles == LAST_TILES:
                    dve.wait_ge(added[LAST_TILES - 1], BATCHES + 1)
            either(dve, narrow, general)


def ffn1(nc, k, g, out):
    X = EXPERTS
    CH = H
    with ExitStack() as ctx:
        a = allocator(nc, ctx)
        wa, wb, wo = (a.sb(n, [P, X, H, D]) for n in ("wa", "wb", "wo"))
        wr = a.sb("wr1", [P, H, X])
        br = a.sb("br1", [P, X])
        bo = a.sb("bo", [X, D])
        bn = a.sb("bn", [P, 4, X * CH])
        y = a.sb("y", [P, NODE_TILES, D])
        gate = a.sb("gate", [P, NODE_TILES, X])
        xn = a.sb("exn", [P, GROUP, D])
        agg = a.sb("agg", [P, D])
        rden = a.sb("rden", [P, HEADS])
        lg, ex, gate_n = (a.sb(n, [P, GROUP, X]) for n in ("lg", "ex", "gate_n"))
        top, total = a.sb("etop", [P, GROUP]), a.sb("etotal", [P, GROUP])
        gate_t = a.sb("gate_t", [X, GROUP, P])
        sums, sums_s = a.sb("esums", [P, H, P]), a.sb("esums_s", [HEADS, P])
        xt = a.sb("ext", [P, H, GCOLS])
        ln = Named()
        ln.stats, ln.mv = a.sb("estats", [P, GROUP, 6]), a.sb("emv", [P, GROUP, 2])
        ln.var, ln.rstd, ln.tmp = (a.sb(f"e{n}", [P, GROUP]) for n in ("var", "rstd", "tmp"))
        h1_both = a.sb("h1", [P, 2, CH, GCOLS])
        h1 = [h1_both[:, i] for i in range(2)]
        flat = h1_both[0:X * CH].rearrange("p a b c -> p (a b c)")
        bn_par = flat[:, 0:10 * P].rearrange("p (i f) -> p i f", f=P)
        bn_t = flat[:, 10 * P:14 * P].rearrange("p (i f) -> p i f", f=P)
        h2 = [a.sb(f"h2_{i}", [P, CH, GCOLS]) for i in range(2)]
        p1 = [a.bank(f"p1_{i}", GCOLS) for i in range(CH)]
        p2 = [a.bank(f"p2_{i}", GCOLS) for i in range(CH)]
        py = [a.bank(f"py_{i}", D) for i in range(2)]
        fin_ps = [a.bank(f"fin_ps{i}", BANK) for i in range(2)]
        w_load, p_load, y_load, y_first = a.sems("w_load", 3), a.sem("p_load"), a.sem("y_load"), a.sem("y_first")
        s, bn_turned, bn_ready = a.sem("esteps"), a.sem("bn_turned"), a.sem("bn_ready")
        bn_steps = a.sem("bn_steps")
        m1, k1, m2, k2 = a.sem("m1s"), a.sem("k1s"), a.sem("m2s"), a.sem("k2s")
        ym, yt = a.sem("ym"), a.sem("yt")
        fetched, sums_turned, sums_read = a.sem("efetched"), a.sem("esums_turned"), a.sem("esums_read")
        xn_turned, xn_kept = a.sem("exn_turned"), a.sem("exn_kept")
        bias_made, bias_added = a.sem("ebias_made"), a.sem("ebias_added")
        xn_made, logits_made, shifted, exp_made = (
            a.sem(f"e_{n}") for n in ("xn_made", "logits_made", "shifted", "exp_made"))
        gates_made, gates_turned, gates_kept = (
            a.sem(f"e_{n}") for n in ("gates_made", "gates_turned", "gates_kept"))
        norm_steps, gate_steps = a.sem("enorm_steps"), a.sem("egate_steps")
        o_sem = a.sem("out_stored")
        block = ctx.enter_context(nc.Block())
        rows16 = "e (c p) -> (e c) p"
        names = ["v1", "g1", "b1", "m1", "be1", "v2", "g2", "b2", "m2", "be2"]
        whole = (NODE_TILES - 1) * P
        SUM_STEPS, GATE_STEPS = 4, 7
        order = []
        for e in range(X + 2):
            order += [(1, e)] * (e < X) + [(2, e - 1)] * (1 <= e <= X) + [(3, e - 2)] * (e >= 2)
        stages = {0: [("fetch", 0)], 1: [("sums", 0), ("fetch", 1)], 2: [("sums", 1), ("fetch", 2)],
                  3: [("sums", 2), ("fetch", 3)], 4: [("sums", 3)], 5: [("norm", None)],
                  7: [("turn", 0)], 8: [("turn", 1)], 9: [("turn", 2)], 10: [("turn", 3)],
                  11: [("logits", None)], 13: [("gates", None)],
                  15: [("bias", 0)], 16: [("bias", 1)], 17: [("bias", 2)], 18: [("bias", 3)]}

        def weave(gi, mine, ahead, piece, fin):
            for i, (layer, e) in enumerate(order):
                if mine:
                    piece(gi, layer, e, mine)
                for stage, t in stages.get(i, []) if ahead else []:
                    if t is None or t < len(ahead):
                        fin(gi + 1, stage, t, ahead)

        def all_groups(eng, piece, fin):
            weave(-1, [], [P] * GROUP, piece, fin)
            with eng.Fori(0, GROUPS - 1) as i:
                weave(i, [P] * GROUP, [P] * GROUP, piece, fin)
            weave(GROUPS - 1, [P] * GROUP, [LAST_ROWS], piece, fin)
            weave(GROUPS, [LAST_ROWS], [], piece, fin)

        def y_count(gi, e, t, mine):
            return GROUP * X * gi + len(mine) * e + t

        @block.sync
        def _(sp):
            sp.dma_start(y[:, 0:GROUP, :], k.x2_d[0:GCOLS, :].rearrange("(t p) d -> p t d", p=P)
                         ).then_inc(y_first, 16)
            for i, n in enumerate(names):
                sp.dma_start(bn_par[:, i, :], g[f"L1_ffn_{n}"].rearrange(rows16, p=P)).then_inc(p_load, 16)
            sp.dma_start(wr[:], g["L1_ffn_Wr"].rearrange("(h p) x -> p h x", p=P)).then_inc(p_load, 16)
            sp.dma_start(br[:], g["L1_ffn_br"].rearrange("(a x) -> a x", a=1).broadcast_to([P, X])
                         ).then_inc(p_load, 16)
            sp.dma_start(bo[:], g["L1_ffn_bo"]).then_inc(p_load, 16)
            for i, (w, n) in enumerate(((wa, "W1"), (wb, "W2"), (wo, "Wo"))):
                for e in range(X):
                    sp.dma_start(w[:, e, :, :], g[f"L1_ffn_{n}"][e].rearrange("(h p) d -> p h d", p=P)
                                 ).then_inc(w_load[i], 16)
                if i == 0:
                    sp.dma_start(y[:, GROUP:NODE_TILES - 1, :], k.x2_d[GCOLS:whole, :].rearrange(
                        "(t p) d -> p t d", p=P)).then_inc(y_load, 16)
                    sp.dma_start(y[:LAST_ROWS, NODE_TILES - 1, :], k.x2_d[whole:N, :]).then_inc(y_load, 16)
            with sp.Fori(0, GROUPS) as gi:
                sp.wait_ge(yt, GROUP * X * gi + GROUP * X + 2)
                sp.dma_start(out[cols(gi * GCOLS, GCOLS), :].rearrange("(t p) d -> p t d", p=P),
                             y[:, cols(gi * GROUP, GROUP), :]).then_inc(o_sem, 16)
            sp.wait_ge(yt, GROUP * X * GROUPS + X + 2)
            sp.dma_start(out[whole:N, :], y[:LAST_ROWS, NODE_TILES - 1, :]).then_inc(o_sem, 16)
            sp.wait_ge(o_sem, 16 * (GROUPS + 1))

        @block.tensor
        def _(pe):
            pe.sem_inc(k1, 2)
            pe.sem_inc(k2, 2)
            pe.sem_inc(yt, 2)
            pe.sem_inc(sums_turned, 1)
            pe.sem_inc(xn_kept, 1)
            pe.sem_inc(bias_added, 1)
            pe.sem_inc(sums_read, 2)
            pe.wait_ge(bn_ready, 1)
            for i in range(4):
                ins = pe.transpose(fin_ps[1][:, i * X * CH:(i + 1) * X * CH], bn_t[:, i, :], k.ident[0:X * CH, 0:X * CH])
            ins.then_inc(bn_turned, 1)
            pe.wait_ge(bn_ready, 2)
            pe.wait_ge(p_load, 16 * 13)

            def fin(gi, stage, t, sizes):
                n, r = GROUP * gi + (t or 0), sizes[0]
                if stage == "sums":
                    bank = fin_ps[t % 2]
                    pe.wait_ge(fetched, n + 1)
                    pe.wait_ge(sums_read, n + 1)
                    pe.wait_ge(bias_added, GROUP * gi + 1)
                    for h in range(H):
                        pe.transpose(bank[:r, h * P:(h + 1) * P], sums[:, h, :r], k.ident[:])
                    pe.transpose(bank[:r, D:D + HEADS], sums_s[:, :r], k.ident[0:HEADS, 0:HEADS]
                                 ).then_inc(sums_turned, 1)
                if stage == "turn":
                    pe.wait_ge(xn_made, gi + 1)
                    pe.wait_ge(xn_kept, n + 1)
                    for h in range(H):
                        ins = pe.transpose(fin_ps[0][:, h * P:h * P + r], xn[:r, t, h * P:(h + 1) * P],
                                           k.ident[:r, :r])
                    ins.then_inc(xn_turned, 1)
                if stage == "logits":
                    pe.wait_ge(xn_kept, n + len(sizes) + 1)
                    for u in range(len(sizes)):
                        for h in range(H):
                            ins = pe.matmul(fin_ps[1][:r, u * X:(u + 1) * X], xt[:, h, u * P:u * P + r], wr[:, h, :],
                                            start=(h == 0), stop=(h == H - 1))
                    ins.then_inc(logits_made, 1)
                if stage == "gates":
                    pe.wait_ge(gates_made, gi + 1)
                    for u in range(len(sizes)):
                        ins = pe.transpose(fin_ps[1][0:X, u * P:u * P + r], gate_n[:r, u, :], k.ident[:r, :r])
                    ins.then_inc(gates_turned, 1)
                if stage == "bias":
                    pe.wait_ge(gates_kept, gi + 1)
                    pe.wait_ge(bias_added, n + 1)
                    pe.matmul(fin_ps[0][:r, 0:D], gate_t[:, t, :r], bo[:], start=True, stop=True
                              ).then_inc(bias_made, 1)

            def piece(gi, layer, e, mine):
                m = sum(mine)
                if e == 0:
                    pe.wait_ge(w_load[layer - 1], 16 * X)
                if layer == 1:
                    if e == 0:
                        pe.wait_ge(xn_kept, GROUP * gi + len(mine) + 1)
                    for c in range(CH):
                        pe.wait_ge(k1, CH * X * gi + CH * e + c + 1)
                        for h in range(H):
                            ins = pe.matmul(p1[c][:, :m], wa[:, e, h, c * P:(c + 1) * P],
                                            k.acc[:, h, cols(gi * GCOLS, m)], start=(h == 0), stop=(h == H - 1))
                        ins.then_inc(m1, 1)
                elif layer == 2:
                    pe.wait_ge(k1, CH * X * gi + CH * e + CH + 2)
                    for c in range(CH):
                        pe.wait_ge(k2, CH * X * gi + CH * e + c + 1)
                        for h in range(CH):
                            ins = pe.matmul(p2[c][:, :m], wb[:, e, h, c * P:(c + 1) * P],
                                            h1[e % 2][:, h, :m], start=(h == 0), stop=(h == CH - 1))
                        ins.then_inc(m2, 1)
                else:
                    pe.wait_ge(k2, CH * X * gi + CH * e + CH + 2)
                    for t, r in enumerate(mine):
                        q = y_count(gi, e, t, mine)
                        pe.wait_ge(yt, q + 1)
                        b = (t if len(mine) > 1 else e) % 2
                        for h in range(CH):
                            ins = pe.matmul(py[b][:r, 0:D], h2[e % 2][:, h, t * P:t * P + r], wo[:, e, h, :],
                                            start=(h == 0), stop=(h == CH - 1))
                        ins.then_inc(ym, 1)

            all_groups(pe, piece, fin)

        @block.scalar
        def _(act):
            act.wait_ge(bn_ready, 2)

            def fin(gi, stage, t, sizes):
                n, r = GROUP * gi + (t or 0), sizes[0]
                here = cols(gi * GCOLS + (t or 0) * P, r)
                if stage == "fetch":
                    act.wait_ge(sums_turned, n + 1)
                    act.copy(sums[:, :, :r], k.acc[:, :, here])
                    act.copy(sums_s[:, :r], k.acc_s[:, here]).then_inc(fetched, 1)
                if stage == "turn":
                    act.wait_ge(xn_turned, n + 1)
                    turned = fin_ps[0][:, 0:D].rearrange("p (h n) -> p h n", h=H)[:, :, :r]
                    act.copy(xt[:, :, t * P:t * P + r], turned)
                    act.copy(k.acc[:, :, here], turned).then_inc(xn_kept, 1)
                if stage == "logits":
                    act.wait_ge(shifted, gi + 1)
                    act.activation(ex[:r, 0:len(sizes), :], lg[:r, 0:len(sizes), :], ACT.Exp).then_inc(exp_made, 1)

            def piece(gi, layer, e, mine):
                m = sum(mine)
                if layer == 3:
                    return
                made, kept, src, dst, j = ((m1, k1, p1, h1, 0), (m2, k2, p2, h2, 2))[layer - 1]
                for c in range(CH):
                    act.wait_ge(made, CH * X * gi + CH * e + c + 1)
                    q = CH * e + c
                    act.activation(dst[e % 2][:, c, :m], src[c][:, :m], ACT.Relu, scale=bn[:, j, q:q + 1],
                                   bias=bn[:, j + 1, q:q + 1]).then_inc(kept, 1)
            all_groups(act, piece, fin)

        @block.vector
        def _(dve):
            st = Steps(dve, bn_steps, 0, k)
            dve.wait_ge(p_load, 16 * 13)
            for j in range(2):
                v = bn_par[:, 5 * j, :]
                st.then(dve.tensor_scalar(v, v, BN_EPS, None, ALU.add))
                inverse_root(dve, st, v, bn_t[:, 2 * j, :], bn_t[:, 2 * j + 1, :])
            for j in range(2):
                _, gam, b, mean, beta = (bn_par[:, 5 * j + i, :] for i in range(5))
                scale, shift = bn_t[:, 2 * j, :], bn_t[:, 2 * j + 1, :]
                st.done(dve.tensor_tensor(shift, b, mean, ALU.subtract))
                st.then(dve.tensor_tensor(scale, scale, gam, ALU.mult))
                st.then(dve.tensor_tensor(shift, shift, scale, ALU.mult))
                st.then(dve.tensor_tensor(shift, shift, beta, ALU.add))
            dve.sem_inc(bn_ready, 1)
            dve.wait_ge(bn_turned, 1)
            st.then(dve.tensor_copy(bn[:].rearrange("p a b -> p (a b)"), fin_ps[1][:, 0:4 * X * CH]))
            dve.sem_inc(bn_ready, 1)
            dve.wait_ge(y_first, 16)

            def fin(gi, stage, t, sizes):
                n, r, m = GROUP * gi + (t or 0), sizes[0], len(sizes)
                if stage in ("sums", "bias"):
                    row = y[:r, cols(n, 1), :].rearrange("p a d -> p (a d)")
                if stage == "sums" and t == 0 and not (isinstance(gi, int) and gi == 0):
                    dve.wait_ge(y_load, 32)
                if stage == "sums":
                    st = Steps(dve, s, SUM_STEPS * n, k)
                    bank = fin_ps[t % 2]
                    dve.wait_ge(sums_turned, n + 2)
                    st.then(dve.tensor_scalar(rden[:r, :], bank[:r, D:D + HEADS], 1e-16, None, ALU.add))
                    st.then(dve.reciprocal(rden[:r, :], rden[:r, :]))
                    st.then(dve.tensor_tensor(
                        agg[:r, :].rearrange("p (h d) -> p h d", h=HEADS),
                        bank[:r, 0:D].rearrange("p (h d) -> p h d", h=HEADS),
                        rden[:r, :].unsqueeze(2).broadcast_to([r, HEADS, HD]), ALU.mult))
                    dve.sem_inc(sums_read, 1)
                    st.then(dve.tensor_tensor(row, row, agg[:r, :], ALU.add))
                    assert st.n == SUM_STEPS
                if stage == "norm":
                    st = Steps(dve, norm_steps, (GROUP_NORM_STEPS + GROUP) * gi, k)
                    x3 = y[:, cols(GROUP * gi, m), :]
                    group_norms(dve, st, k, x3, ln, sizes)
                    for u in range(m):
                        st.done(dve.tensor_scalar(xn[:r, u, :], x3[:r, u, :], ln.mv[:r, u, 0:1],
                                                  ln.rstd[:r, u:u + 1], ALU.subtract, ALU.mult))
                    st.wait()
                    dve.sem_inc(xn_made, 1)
                if stage == "logits":
                    st = Steps(dve, gate_steps, GATE_STEPS * gi, k)

                    def each(v, width):
                        return v.unsqueeze(2).broadcast_to([r, m, width])
                    dve.wait_ge(logits_made, gi + 1)
                    st.then(dve.tensor_tensor(
                        lg[:r, 0:m, :], fin_ps[1][:r, 0:m * X].rearrange("p (t x) -> p t x", x=X),
                        br[:r, :].unsqueeze(1).broadcast_to([r, m, X]), ALU.add))
                    st.then(dve.tensor_reduce(top[:r, 0:m], lg[:r, 0:m, :], AX, ALU.max))
                    st.then(dve.tensor_tensor(lg[:r, 0:m, :], lg[:r, 0:m, :], each(top[:r, 0:m], X), ALU.subtract))
                    dve.sem_inc(shifted, 1)
                    dve.wait_ge(exp_made, gi + 1)
                    st.then(dve.tensor_reduce(total[:r, 0:m], ex[:r, 0:m, :], AX, ALU.add))
                    st.then(dve.reciprocal(total[:r, 0:m], total[:r, 0:m]))
                    st.done(dve.tensor_tensor(gate[:r, cols(GROUP * gi, m), :], ex[:r, 0:m, :],
                                              each(total[:r, 0:m], X), ALU.mult))
                    st.then(dve.tensor_tensor(gate_n[:r, 0:m, :], ex[:r, 0:m, :], each(total[:r, 0:m], X), ALU.mult))
                    assert st.n == GATE_STEPS
                    dve.sem_inc(gates_made, 1)
                if stage == "gates":
                    dve.wait_ge(gates_turned, gi + 1)
                    dve.tensor_copy(gate_t[:, 0:m, :r], fin_ps[1][0:X, 0:m * P].rearrange(
                        "x (t p) -> x t p", p=P)[:, :, :r]).then_inc(gates_kept, 1)
                if stage == "bias":
                    dve.wait_ge(bias_made, n + 1)
                    dve.tensor_tensor(row, row, fin_ps[0][:r, 0:D], ALU.add).then_inc(bias_added, 1)

            def piece(gi, layer, e, mine):
                if layer != 3:
                    return
                for t, r in enumerate(mine):
                    n = GROUP * gi + t
                    q = y_count(gi, e, t, mine)
                    b = (t if len(mine) > 1 else e) % 2
                    dve.wait_ge(ym, q + 1)
                    if e == 0:
                        if t == 0:
                            dve.wait_ge(bias_added, GROUP * gi + len(mine) + 1)
                    else:
                        dve.wait_ge(yt, q - len(mine) + 3)
                    row = y[:r, cols(n, 1), :].rearrange("p a d -> p (a d)")
                    dve.scalar_tensor_tensor(row, py[b][:r, 0:D], gate[:r, cols(n, 1), e:e + 1].rearrange(
                        "p a x -> p (a x)"), row, ALU.mult, ALU.add).then_inc(yt, 1)
            all_groups(dve, piece, fin)


def build(nc, g, out):
    with ExitStack() as ctx:
        a = allocator(nc, ctx)
        k = Named()

        def dram(name, shape, dt=F32):
            return nc.dram_tensor(name, shape, dt, kind="Internal").ap()
        k.table0_d = dram("table0", (RELS * NP, D))
        k.table1_d = dram("table1", (N, ROW1))
        k.x1_d, k.x2_d = dram("x1", (NP, D)), dram("x2", (NP, D))
        k.starts_d = dram("starts_d", (HEADS, TPAD, P + 1))
        k.ends_d, k.both_d = dram("ends_d", (TPAD, 2)), dram("both_d", (TPAD,))
        k.base_d, k.base_f_d = dram("base_d", (TPAD,), I32), dram("base_f_d", (TPAD,))

        k.acc = a.sb("acc", [P, H, COLS])
        k.acc_s = a.sb("acc_s", [HEADS, COLS])
        k.got0, k.got1 = a.sems("got0_", 2 * BT), a.sems("got1_", 2 * BT)
        k.xload0, k.xload1 = a.sems("xload0_", 2), a.sems("xload1_", 2)
        k.starts_stored = a.sem("starts_stored")
        k.passed = a.sem("passed")
        k.ident, k.iota = a.sb("ident", [P, P]), a.sb("iota", [P, P])
        k.head_of, k.head_of_t = a.sb("head_of", [P, HEADS]), a.sb("head_of_t", [HEADS, P])
        k.tile_of, k.head_rows = a.sb("tile_of", [P, BT]), a.sb("head_rows", [HEADS, D])
        k.ones = a.sb("ones", [1, P])
        k.eps, k.unused = a.sb("eps", [P, 1]), a.sb("unused", [P, 1])
        k.node_sums = a.sb("node_sums", [P, H, NODE_TILES])
        constants(nc, k)
        with ExitStack() as graph:
            b = allocator(nc, graph)
            k.meta = b.sb("meta", [P, 4, TPAD])
            k.base = b.sb("base", [1, BT + TPAD], I32)
            k.near = b.sb("near", [P, TPAD])
            k.narrow = b.sb("narrow", [1, 1], I32)
            k.ends8, k.both8 = b.sb("ends8", [HEADS, 2 * TPAD]), b.sb("both8", [HEADS, TPAD])
            with ExitStack() as stored_late:
                k.starts = allocator(nc, stored_late).sb("starts", [P, BLOCKS, P + 1])
                edge_tables(nc, k, g)
                relation_table(nc, k, g)
            gnn0_edges(nc, k)
            gnn0_nodes(nc, k, g)
            with ExitStack() as experts:
                c = allocator(nc, experts)
                k.w1 = c.sb("w1", [P, 2, H, F0])
                k.w2 = c.sb("w2", [P, 2, F0 // P, D])
                k.b1, k.b2 = c.sb("b1", [P, 2, F0 // P]), c.sb("b2", [1, D])
                route(nc, k, g)
                ffn0(nc, k, g)
            gnn1_edges(nc, k)
        ffn1(nc, k, g, out)


NAMES = ["x", "src", "dst", "edge_type_8", "edge_weight", "L0_gnn_weight", "L0_ffn_Wr", "L0_ffn_br",
         "L0_ffn_W1", "L0_ffn_b1", "L0_ffn_W2", "L0_ffn_b2", "L0_ffn_gamma", "L0_ffn_beta", "L1_gnn_W",
         "L1_gnn_a_src", "L1_gnn_a_dst", "L1_ffn_Wr", "L1_ffn_br", "L1_ffn_W1", "L1_ffn_b1", "L1_ffn_g1",
         "L1_ffn_be1", "L1_ffn_m1", "L1_ffn_v1", "L1_ffn_W2", "L1_ffn_b2", "L1_ffn_g2", "L1_ffn_be2",
         "L1_ffn_m2", "L1_ffn_v2", "L1_ffn_Wo", "L1_ffn_bo"]


def kernel(**inputs):
    import concourse.bacc as bacc
    from concourse.bass_utils import run_bass_kernel_spmd

    nc = bacc.Bacc("TRN2", target_bir_lowering=False, num_devices=1)
    arrays, g = {}, {}
    for name in NAMES:
        arr = np.ascontiguousarray(inputs[name])
        arrays[f"in_{name}"] = arr
        g[name] = nc.dram_tensor(f"in_{name}", arr.shape, mybir.dt.from_np(arr.dtype), kind="ExternalInput").ap()
    out = nc.dram_tensor("out", (N, D), F32, kind="ExternalOutput").ap()
    build(nc, g, out)
    r = run_bass_kernel_spmd(nc, [arrays], core_ids=[0])
    return r.results[0]["out"]
```
